# Optimizing a Trainium2 kernel written in Bass

```python
import numpy as np
import jax
import jax.numpy as jnp

def _softmax(x, axis=-1):
    return jax.nn.softmax(x, axis=axis)

def _gelu(x):
    return jax.nn.gelu(x, approximate=True)

def _silu(x):
    return jax.nn.silu(x)

def _sigmoid(x):
    return jax.nn.sigmoid(x)

def _layernorm(x, axis=-1, eps=1e-05):
    m = jnp.mean(x, axis=axis, keepdims=True)
    v = jnp.var(x, axis=axis, keepdims=True)
    return (x - m) / jnp.sqrt(v + eps)

def _scatter_add(tgt, idx, src, axis=0):
    return tgt.at[idx].add(src)

def _segment_sum(src, seg, n):
    return jax.ops.segment_sum(src, seg, n)
kernel_name = 'mk_decoder_preln_d1_seqx_r4_0616a1'

def setup_inputs(seed: int=0):
    np.random.seed(seed)
    _w = jnp.asarray

    def _rec_inputs():
        import jax
        import jax.numpy as jnp
        _rk = jax.random.key(seed)
        x = -0.0002928 + 1 * jax.random.normal(jax.random.fold_in(_rk, 1), (32, 128, 512), jnp.float32)
        _lenS = 128 - jax.random.randint(jax.random.fold_in(_rk, 7), (32,), 0, max(1, 128 // 4) + 1, jnp.int32)
        _lenS2 = 128 - jax.random.randint(jax.random.fold_in(_rk, 8), (32,), 0, max(1, 128 // 4) + 1, jnp.int32)
        _ctx_2048P = jax.random.normal(jax.random.fold_in(_rk, 11), (32, 16, 512), jnp.float32)
        _ctx_2048c = jax.random.dirichlet(jax.random.fold_in(_rk, 511), 0.3 * jnp.ones((16,), jnp.float32), (32, 128))
        _ctx_2048t = jnp.einsum('bsk,bkd->bsd', _ctx_2048c, _ctx_2048P)
        _ctx_2048t = _ctx_2048t * jax.lax.rsqrt(jnp.mean(jnp.square(_ctx_2048t)) + 1e-12) * 0.953939
        ctx_2048 = -1.39393e-06 + 0.999914 * (_ctx_2048t + 0.3 * jax.random.normal(jax.random.fold_in(_rk, 611), (32, 128, 512), jnp.float32))
        return (x, ctx_2048)
    x, ctx_2048 = _rec_inputs()

    def _L0_attn_setup():
        import jax, jax.numpy as jnp
        import numpy as np
        import math
        E = 512
        H = 16
        HD = E // H // 2
        DEPTH = 12
        LAMBDA_INIT = 0.8 - 0.6 * math.exp(-0.3 * DEPTH)
        key = jax.random.key(seed)
        ks = jax.random.split(key, 9)
        s = 0.02
        return {'x': jax.random.normal(ks[0], (2, 512, E), jnp.float32), 'Wq': jax.random.normal(ks[1], (E, E), jnp.float32) * s, 'Wk': jax.random.normal(ks[2], (E, E), jnp.float32) * s, 'Wv': jax.random.normal(ks[3], (E, E), jnp.float32) * s, 'Wo': jax.random.normal(ks[4], (E, E), jnp.float32) * s, 'lq1': jax.random.normal(ks[5], (HD,), jnp.float32) * 0.1, 'lk1': jax.random.normal(ks[6], (HD,), jnp.float32) * 0.1, 'lq2': jax.random.normal(ks[7], (HD,), jnp.float32) * 0.1, 'lk2': jax.random.normal(ks[8], (HD,), jnp.float32) * 0.1}
    _L0_attn_all = _L0_attn_setup()
    _L0_attn_in = {k: v for k, v in _L0_attn_all.items() if k in ('Wq', 'Wk', 'Wv', 'Wo', 'lq1', 'lk1', 'lq2', 'lk2')}
    del _L0_attn_all

    def _L0_xattn_setup():
        import math
        import jax, jax.numpy as jnp
        import numpy as np
        N_HEADS = 8
        CHANNELS = 128
        K_CH = CHANNELS // N_HEADS
        THETA = 10000.0

        def _rope_freqs(length, dim):
            inv_freq = 1.0 / THETA ** (jnp.arange(0, dim, 2, dtype=jnp.float32) / dim)
            f = jnp.arange(length, dtype=jnp.float32)[:, None] * inv_freq[None, :]
            return jnp.concatenate([f, f], axis=-1)

        def _apply_rotary(pos, t):
            half = t.shape[-1] // 2
            rot = jnp.concatenate([-t[..., half:], t[..., :half]], axis=-1)
            return t * jnp.cos(pos) + rot * jnp.sin(pos)

        def _proj(inp, W, b):
            return jnp.einsum('oc,bct->bot', W, inp) + b[None, :, None]
        key = jax.random.key(seed)
        ks = jax.random.split(key, 10)
        B, C, T = (4, CHANNELS, 512)
        bound = math.sqrt(6.0 / (C + C))

        def w(k):
            return jax.random.uniform(k, (C, C), jnp.float32, -bound, bound)
        return {'x': jax.random.normal(ks[0], (B, C, T), jnp.float32), 'c': jax.random.normal(ks[1], (B, C, T), jnp.float32), 'Wq': w(ks[2]), 'bq': jnp.zeros((C,), jnp.float32), 'Wk': w(ks[3]), 'bk': jnp.zeros((C,), jnp.float32), 'Wv': w(ks[4]), 'bv': jnp.zeros((C,), jnp.float32), 'Wo': w(ks[5]), 'bo': jnp.zeros((C,), jnp.float32)}
    _L0_xattn_all = _L0_xattn_setup()
    _L0_xattn_in = {k: v for k, v in _L0_xattn_all.items() if k in ('Wq', 'bq', 'Wk', 'bk', 'Wv', 'bv', 'Wo', 'bo')}
    del _L0_xattn_all

    def _L0_ffn_setup():
        import jax, jax.numpy as jnp
        import numpy as np
        NUM_EXPERTS = 32
        TOP_K = 6
        N_GROUPS = 4
        N_LIMITED_GROUPS = 2
        key = jax.random.key(seed)
        ks = jax.random.split(key, 8)
        H, M = (512, 352)
        SH = 2 * M
        s = 0.02
        return {'hidden_states': jax.random.normal(ks[0], (4, 512, H), jnp.float32), 'gate_w': jax.random.normal(ks[1], (H, NUM_EXPERTS), jnp.float32) * s, 'w_gate': jax.random.normal(ks[2], (NUM_EXPERTS, H, M), jnp.float32) * s, 'w_up': jax.random.normal(ks[3], (NUM_EXPERTS, H, M), jnp.float32) * s, 'w_down': jax.random.normal(ks[4], (NUM_EXPERTS, M, H), jnp.float32) * s, 'sw_gate': jax.random.normal(ks[5], (H, SH), jnp.float32) * s, 'sw_up': jax.random.normal(ks[6], (H, SH), jnp.float32) * s, 'sw_down': jax.random.normal(ks[7], (SH, H), jnp.float32) * s}
    _L0_ffn_all = _L0_ffn_setup()
    _L0_ffn_in = {k: v for k, v in _L0_ffn_all.items() if k in ('gate_w', 'w_gate', 'w_up', 'w_down', 'sw_gate', 'sw_up', 'sw_down')}
    del _L0_ffn_all
    return {'x': x, 'ctx_2048': ctx_2048, 'L0_attn_Wq': _L0_attn_in['Wq'], 'L0_attn_Wk': _L0_attn_in['Wk'], 'L0_attn_Wv': _L0_attn_in['Wv'], 'L0_attn_Wo': _L0_attn_in['Wo'], 'L0_attn_lq1': _L0_attn_in['lq1'], 'L0_attn_lk1': _L0_attn_in['lk1'], 'L0_attn_lq2': _L0_attn_in['lq2'], 'L0_attn_lk2': _L0_attn_in['lk2'], 'L0_xattn_Wq': _L0_xattn_in['Wq'], 'L0_xattn_bq': _L0_xattn_in['bq'], 'L0_xattn_Wk': _L0_xattn_in['Wk'], 'L0_xattn_bk': _L0_xattn_in['bk'], 'L0_xattn_Wv': _L0_xattn_in['Wv'], 'L0_xattn_bv': _L0_xattn_in['bv'], 'L0_xattn_Wo': _L0_xattn_in['Wo'], 'L0_xattn_bo': _L0_xattn_in['bo'], 'L0_ffn_gate_w': _L0_ffn_in['gate_w'], 'L0_ffn_w_gate': _L0_ffn_in['w_gate'], 'L0_ffn_w_up': _L0_ffn_in['w_up'], 'L0_ffn_w_down': _L0_ffn_in['w_down'], 'L0_ffn_sw_gate': _L0_ffn_in['sw_gate'], 'L0_ffn_sw_up': _L0_ffn_in['sw_up'], 'L0_ffn_sw_down': _L0_ffn_in['sw_down']}

def reference(x, ctx_2048, L0_attn_Wq, L0_attn_Wk, L0_attn_Wv, L0_attn_Wo, L0_attn_lq1, L0_attn_lk1, L0_attn_lq2, L0_attn_lk2, L0_xattn_Wq, L0_xattn_bq, L0_xattn_Wk, L0_xattn_bk, L0_xattn_Wv, L0_xattn_bv, L0_xattn_Wo, L0_xattn_bo, L0_ffn_gate_w, L0_ffn_w_gate, L0_ffn_w_up, L0_ffn_w_down, L0_ffn_sw_gate, L0_ffn_sw_up, L0_ffn_sw_down):
    import jax
    import jax.numpy as jnp

    def _L0_attn_ref(x, Wq, Wk, Wv, Wo, lq1, lk1, lq2, lk2):
        import jax, jax.numpy as jnp
        import numpy as np
        import math
        E = 512
        H = 16
        HD = E // H // 2
        DEPTH = 12
        LAMBDA_INIT = 0.8 - 0.6 * math.exp(-0.3 * DEPTH)
        b, t, e = x.shape
        scaling = HD ** (-0.5)
        q = (x @ Wq).reshape(b, t, 2 * H, HD).transpose(0, 2, 1, 3) * scaling
        k = (x @ Wk).reshape(b, t, 2 * H, HD).transpose(0, 2, 1, 3)
        v = (x @ Wv).reshape(b, t, H, 2 * HD).transpose(0, 2, 1, 3)
        scores = jnp.einsum('bhqd,bhkd->bhqk', q, k)
        causal = jnp.triu(jnp.full((t, t), -jnp.inf, dtype=jnp.float32), 1)
        aw = jax.nn.softmax((scores + causal).astype(jnp.float32), axis=-1)
        lam = jnp.exp(jnp.sum(lq1 * lk1)) - jnp.exp(jnp.sum(lq2 * lk2)) + LAMBDA_INIT
        aw = aw.reshape(b, H, 2, t, t)
        aw = aw[:, :, 0] - lam * aw[:, :, 1]
        attn = jnp.einsum('bhqk,bhkd->bhqd', aw, v)
        attn = attn * jax.lax.rsqrt(jnp.mean(attn * attn, axis=-1, keepdims=True) + 1e-05)
        attn = attn * (1.0 - LAMBDA_INIT)
        attn = attn.transpose(0, 2, 1, 3).reshape(b, t, H * 2 * HD)
        return attn @ Wo

    def _L0_xattn_ref(x, c, Wq, bq, Wk, bk, Wv, bv, Wo, bo):
        import math
        import jax, jax.numpy as jnp
        import numpy as np
        N_HEADS = 8
        CHANNELS = 128
        K_CH = CHANNELS // N_HEADS
        THETA = 10000.0

        def _rope_freqs(length, dim):
            inv_freq = 1.0 / THETA ** (jnp.arange(0, dim, 2, dtype=jnp.float32) / dim)
            f = jnp.arange(length, dtype=jnp.float32)[:, None] * inv_freq[None, :]
            return jnp.concatenate([f, f], axis=-1)

        def _apply_rotary(pos, t):
            half = t.shape[-1] // 2
            rot = jnp.concatenate([-t[..., half:], t[..., :half]], axis=-1)
            return t * jnp.cos(pos) + rot * jnp.sin(pos)

        def _proj(inp, W, b):
            return jnp.einsum('oc,bct->bot', W, inp) + b[None, :, None]
        b, _, t_t = x.shape
        t_s = c.shape[2]
        q_emb = _rope_freqs(t_t, K_CH)
        k_emb = _rope_freqs(t_s, K_CH)

        def split_heads(t):
            return t.reshape(b, N_HEADS, K_CH, t.shape[2]).transpose(0, 1, 3, 2)
        q = split_heads(_proj(x, Wq, bq))
        k = split_heads(_proj(c, Wk, bk))
        v = split_heads(_proj(c, Wv, bv))
        q = _apply_rotary(q_emb, q)
        k = _apply_rotary(k_emb, k)
        scores = jnp.einsum('bhtc,bhsc->bhts', q, k) / math.sqrt(K_CH)
        p_attn = jax.nn.softmax(scores, axis=-1)
        out = jnp.einsum('bhts,bhsc->bhtc', p_attn, v)
        out = out.transpose(0, 1, 3, 2).reshape(b, N_HEADS * K_CH, t_t)
        return _proj(out, Wo, bo)

    def _L0_ffn_ref(hidden_states, gate_w, w_gate, w_up, w_down, sw_gate, sw_up, sw_down):
        import jax, jax.numpy as jnp
        import numpy as np
        NUM_EXPERTS = 32
        TOP_K = 6
        N_GROUPS = 4
        N_LIMITED_GROUPS = 2
        B, S, H = hidden_states.shape
        E, K = (NUM_EXPERTS, TOP_K)
        x = hidden_states.reshape(-1, H)
        T = x.shape[0]
        scores = jax.nn.sigmoid(x @ gate_w)
        original_scores = scores
        epg = E // N_GROUPS
        sg = scores.reshape(T, N_GROUPS, epg)
        group_scores = jnp.max(sg, axis=-1)
        _, top_groups = jax.lax.top_k(group_scores, N_LIMITED_GROUPS)
        mask = jnp.ones((T, N_GROUPS), dtype=bool)
        mask = mask.at[jnp.arange(T)[:, None], top_groups].set(False)
        sg = jnp.where(mask[:, :, None], -jnp.inf, sg)
        masked_scores = sg.reshape(T, E)
        _, selected_experts = jax.lax.top_k(masked_scores, K)
        weights = jnp.take_along_axis(original_scores, selected_experts, axis=-1)
        weights = weights / jnp.sum(weights, axis=-1, keepdims=True)
        sel_flat = selected_experts.ravel()
        x_exp = jnp.repeat(x, K, axis=0)
        sort_idx = jnp.argsort(sel_flat)
        xs = x_exp[sort_idx]
        group_sizes = jnp.bincount(sel_flat, length=E).astype(jnp.int32)
        g = jax.lax.ragged_dot(xs, w_gate, group_sizes)
        u = jax.lax.ragged_dot(xs, w_up, group_sizes)
        d = jax.lax.ragged_dot(jax.nn.silu(g) * u, w_down, group_sizes)
        unsort_idx = jnp.argsort(sort_idx)
        out = d[unsort_idx].reshape(T, K, H)
        expert_out = jnp.sum(out * weights[..., None], axis=1)
        shared = jax.nn.silu(x @ sw_gate) * (x @ sw_up) @ sw_down
        return (expert_out + shared).reshape(B, S, H)
    x = x + _L0_attn_ref(_layernorm(x, axis=-1), L0_attn_Wq, L0_attn_Wk, L0_attn_Wv, L0_attn_Wo, L0_attn_lq1, L0_attn_lk1, L0_attn_lq2, L0_attn_lk2)
    x = x + _L0_xattn_ref(_layernorm(x, axis=-1), ctx_2048, L0_xattn_Wq, L0_xattn_bq, L0_xattn_Wk, L0_xattn_bk, L0_xattn_Wv, L0_xattn_bv, L0_xattn_Wo, L0_xattn_bo)
    x = x + _L0_ffn_ref(_layernorm(x, axis=-1), L0_ffn_gate_w, L0_ffn_w_gate, L0_ffn_w_up, L0_ffn_w_down, L0_ffn_sw_gate, L0_ffn_sw_up, L0_ffn_sw_down)
    return x

_drawn_inputs = setup_inputs


def setup_inputs(seed=0):
    import zlib

    import numpy as np

    out = dict(_drawn_inputs(seed))
    spreads = {'L0_xattn_bq': (0.0, 0.329),
     'L0_xattn_bk': (0.0, 0.64),
     'L0_xattn_bv': (0.0, 0.1),
     'L0_xattn_bo': (0.0, 0.1)}
    factors = {'L0_attn_lq1': 8.0,
     'L0_attn_lq2': 8.0,
     'L0_attn_lk2': 8.0,
     'L0_ffn_gate_w': 3.902,
     'L0_ffn_w_gate': 3.587,
     'L0_ffn_w_up': 3.513,
     'L0_ffn_w_down': 3.516}
    for name, (base, spread) in spreads.items():
        noise = np.random.default_rng([zlib.crc32(name.encode()), seed]).standard_normal(out[name].shape)
        drawn = base * np.exp(spread * noise) if base else spread * noise
        out[name] = jnp.asarray(drawn.astype(out[name].dtype))
    for name, factor in factors.items():
        out[name] = (out[name] * factor).astype(out[name].dtype)
    return out
```

```python
import math
import numpy as np
import concourse.bass as bass
from concourse import mybir
from contextlib import ExitStack

NB = 32
BLK = 256
NBLK = 127
NSLOT = NBLK * BLK
LAMBDA_INIT = 0.8 - 0.6 * math.exp(-0.3 * 12)
BIG = 3.0e38
C_ID, C_TRI, C_ONE, C_SEL, C_COS, C_SIN, C_MSK, C_AB, C_BI = 0, 128, 256, 384, 512, 1024, 1536, 1664, 1666
C_N = C_BI + 128


class Plan:

    def __init__(self):
        self.lists = {n: [] for n in ("pe", "act", "dve", "pool", "sp")}
        self.count = {}
        self.base = {n: [] for n in self.lists}

    def put(self, eng, fn, *after, sem=None, by=1):
        key = sem or eng
        self.count[key] = self.count.get(key, 0) + by
        self.lists[eng].append((self.base[eng] + list(after), fn, key, by))
        self.base[eng] = []
        return (key, self.count[key])

    def quiet(self, eng, fn, *after):
        self.lists[eng].append((self.base[eng] + list(after), fn, None, 0))
        self.base[eng] = []

    def fence(self, *tokens):
        for n in self.base:
            self.base[n] = list(tokens)

    def last(self, *keys):
        return [(k, self.count[k]) for k in keys if self.count.get(k)]

    def emit(self, name, eng, sems):
        seen = {}
        for after, fn, key, by in self.lists[name]:
            for t in after:
                if t is not None and seen.get(t[0], 0) < t[1]:
                    eng.wait_ge(sems[t[0]], t[1])
                    seen[t[0]] = t[1]
            ins = fn(eng)
            if key:
                ins.then_inc(sems[key], by)


def build(nc, I, out):
    f32, bf16, i32 = mybir.dt.float32, mybir.dt.bfloat16, mybir.dt.int32
    ALU, ACT, AX = mybir.AluOpType, mybir.ActivationFunctionType, mybir.AxisListType
    P = Plan()

    def pe(fn, *a): return P.put("pe", fn, *a)
    def act(fn, *a): return P.put("act", fn, *a)
    def dve(fn, *a): return P.put("dve", fn, *a)
    def pool(fn, *a): return P.put("pool", fn, *a)
    def load(sem, dst, src, *a, eng="sp"):
        return P.put(eng, lambda e: e.dma_start(dst, src), *a, sem=sem, by=16)

    top = ExitStack()
    with top:
        def sb(stack, name, shape, dt=f32):
            return stack.enter_context(nc.sbuf_tensor(name, shape, dt))

        XS = nc.dram_tensor("xs_sorted", (NSLOT, 512), f32, kind="Internal").ap()
        YS = nc.dram_tensor("ys_sorted", (NSLOT, 512), f32, kind="Internal").ap()

        ps = top.enter_context(nc.psum_tensor("ps", [128, 8 * 512], f32))

        def bank(i, a=0, b=512):
            return ps[:, i * 512 + a:i * 512 + b]

        X = sb(top, "X", [128, NB, 512])
        CST = sb(top, "CST", [128, C_N])
        ident = CST[:, C_ID:C_ID + 128]
        LG = sb(top, "LG", [128, NB, 32])
        ST3 = sb(top, "ST3", [128, NB, 2])
        NR3 = sb(top, "NR3", [128, 1])
        F = [None] * 8

        t_cst = load("d_cst", CST[:, :], I["cst"])
        mh = sb(top, "mh", [128, 16])
        t_mh = pool(lambda e: e.memset(mh[:, :], -0.5))

        ax = ExitStack()
        WA = sb(ax, "WA", [128, 4, 4, 512])
        WX = sb(ax, "WX", [128, 8, 128])
        WV = sb(ax, "WV", [128, 256])
        WO = sb(ax, "WO", [128, 2, 128])
        BX = sb(ax, "BX", [128, 11])
        GW = sb(ax, "GW", [128, 4, 32])
        LQ = sb(ax, "LQ", [128, 4, 16])
        idb = sb(ax, "idb", [128, 128], bf16)
        mkb = sb(ax, "mkb", [128, 4, 128], bf16)
        zt = sb(ax, "zt", [128, 1024])
        for n, w in enumerate(("Wq", "Wk", "Wv", "Wo")):
            load("d_w", WA[:, n, :, :], I[w].rearrange("(c p) n -> p c n", p=128))
        load("d_w", WX[:, :, :], I["wx"])
        load("d_w", WV[:, :], I["wv"])
        load("d_w", WO[:, :, :], I["wo"])
        load("d_w", BX[:, :], I["bx"])
        load("d_w", GW[:, :, :], I["gate_w"].rearrange("(p c) n -> p c n", c=4))
        t_w = load("d_w", LQ[:, :, :], I["lq"].partition_broadcast(128))

        t_idb = dve(lambda e: e.tensor_copy(idb[:, :], ident), t_cst)
        t_mkb = dve(lambda e: e.tensor_copy(
            mkb[:, :, :], CST[:, C_MSK:C_MSK + 128].unsqueeze(1).broadcast_to([128, 4, 128])), t_cst)
        lm = sb(ax, "lm", [128, 2, 16])
        ls = sb(ax, "ls", [128, 2])
        le = sb(ax, "le", [128, 2])
        neglam = sb(ax, "neglam", [128, 1])
        t = dve(lambda e: e.tensor_tensor(lm[:, :, :], LQ[:, 0:4:2, :], LQ[:, 1:4:2, :], ALU.mult), t_w)
        t = dve(lambda e: e.tensor_reduce(ls[:, :], lm[:, :, :], AX.X, ALU.add), t)
        t = act(lambda e: e.activation(le[:, :], ls[:, :], ACT.Exp), t)
        t = dve(lambda e: e.tensor_tensor(neglam[:, :], le[:, 1:2], le[:, 0:1], ALU.subtract), t)
        t_lam = dve(lambda e: e.tensor_scalar(neglam[:, :], neglam[:, :], -LAMBDA_INIT, None, ALU.add), t)

        t_z = pool(lambda e: e.memset(zt[:, :], 0.0))
        zrows = XS.rearrange("(n p a) d -> n p (a d)", p=128, a=2)

        st6 = sb(ax, "st6", [128, 2, 6])
        mv = sb(ax, "mv", [128, 2, 2])
        ve = sb(ax, "ve", [128, 2, 1])
        lnfree = [None, None]

        def norm(x, dst, which, stats, *after):
            s, m, v = st6[:, which, :], mv[:, which, :], ve[:, which, :]
            t = dve(lambda e: e.bn_stats(s, x), *after, lnfree[which])
            t = dve(lambda e: e.bn_aggr(m, s), t)
            t = pool(lambda e: e.tensor_scalar(v, m[:, 1:2], 1e-5, None, ALU.add), t, t_mh)
            t = pool(lambda e: e.tensor_tensor(stats[:, 1:2], v, mh[:, 0:1], ALU.pow), t)
            t = pool(lambda e: e.tensor_copy(stats[:, 0:1], m[:, 0:1]), t)
            t = pool(lambda e: e.tensor_scalar(dst, x, stats[:, 0:1], stats[:, 1:2], ALU.subtract, ALU.mult), t)
            lnfree[which] = t
            return t

        def turn(src, b, *after):
            def go(e):
                for c in range(4):
                    m = e.transpose(bank(b, 128 * c, 128 * c + 128), src(c), ident)
                return m
            return pe(go, F[b], *after, t_cst)

        xn = sb(ax, "xn", [128, 512])
        sA = sb(ax, "sA", [128, 2])
        xT = sb(ax, "xT", [128, 4, 128])
        qA = sb(ax, "qA", [128, 4, 128])
        qB = sb(ax, "qB", [128, 4, 128])
        kT = sb(ax, "kT", [128, 4, 128])
        vA = sb(ax, "vA", [128, 512])
        nm = sb(ax, "nm", [128, 8])
        nb4 = sb(ax, "nb4", [128, 8])
        PA = sb(ax, "PA", [128, 8, 128])
        SU = sb(ax, "SU", [128, 32])
        RS = sb(ax, "RS", [128, 4, 4])
        CC = sb(ax, "CC", [128, 4, 4])
        aw = sb(ax, "aw", [128, 4, 128])
        awT = sb(ax, "awT", [128, 4, 128])
        R1 = sb(ax, "R1", [128, 4, 4])
        OA = sb(ax, "OA", [128, 16, 32])
        SQ = sb(ax, "SQ", [128, 16, 32])
        MS = sb(ax, "MS", [128, 16])
        MR = sb(ax, "MR", [128, 16])
        oT = sb(ax, "oT", [128, 4, 128])
        xl = {}
        x1 = {}
        x2 = {}
        A = {}

        def load_x(b):
            xl[b] = load(f"d_x{b % 4}", X[:, b, :], I["x"][b, :, :], xl.get(b - 4))

        def chainA(b):
            x = X[:, b, :]
            t_xn = norm(x, xn[:, :], 0, sA, xl[b], A.get("xn"))
            tt = turn(lambda c: xn[:, 128 * c:128 * c + 128], 0, t_xn)
            A["xn"] = tt
            t_xT = act(lambda e: e.activation(xT[:, :, :], bank(0), ACT.Copy), tt, A.get("xT"))
            F[0] = t_xT
            yield

            def proj(b_, w):
                def go(e):
                    for ct in range(4):
                        for c in range(4):
                            m = e.matmul(bank(b_, 128 * ct, 128 * ct + 128),
                                         WA[:, w, c, 128 * ct:128 * ct + 128], xT[:, c, :],
                                         start=(c == 0), stop=(c == 3))
                    return m
                return pe(go, F[b_], t_xT, t_w)

            tq = proj(1, 0)
            t1 = act(lambda e: e.activation(qA[:, :, :], bank(1), ACT.Copy, scale=CST[:, C_AB:C_AB + 1]),
                     tq, A.get("s"))
            t2 = dve(lambda e: e.tensor_scalar(qB[:, :, :], bank(1), CST[:, C_AB + 1:C_AB + 2], None, ALU.mult),
                     tq, t1, A.get("s"))
            F[1] = t2
            yield
            tk = proj(2, 1)
            t3 = act(lambda e: e.activation(kT[:, :, :], bank(2), ACT.Copy), tk, A.get("s"))
            F[2] = t3

            def pv_(e):
                for c in range(4):
                    m = e.matmul(bank(0), xT[:, c, :], WA[:, 2, c, :], start=(c == 0), stop=(c == 3))
                return m
            tv = pe(pv_, F[0], t_xT)
            A["xT"] = tv
            t4 = act(lambda e: e.activation(vA[:, :], bank(0), ACT.Copy), tv, A.get("pv"))
            F[0] = t4
            yield
            for u in range(4):
                def sc(e, u=u):
                    for r in range(2):
                        e.matmul(bank(1 + r), idb[:, :], mkb[:, :, :], start=True, stop=False,
                                 skip_group_check=True)
                    for i in range(2):
                        for hf in range(2):
                            for r in range(2):
                                q, j, ct = (qB if hf else qA), 2 * (u % 2) + r, 2 * (u // 2) + i
                                col = i * 256 + hf * 128
                                m = e.matmul(bank(1 + r, col, col + 128), q[32 * j:32 * j + 32, ct, :],
                                             kT[32 * j:32 * j + 32, ct, :], start=False,
                                             stop=i == 1 and hf == 1, skip_group_check=True)
                    return m
                ts = pe(sc, F[1], F[2], t1, t2, t3, t_idb, t_mkb)
                A["s"] = ts
                S = ps[:, 512:1536].rearrange("p (h k) -> p h k", k=128)
                tm = dve(lambda e: e.tensor_reduce(nm[:, :], S, AX.X, ALU.max, negate=True), ts, A.get("nm"))
                tm = dve(lambda e: e.tensor_scalar(nb4[:, :], nm[:, :], 0.25, None, ALU.mult), tm, A.get("nb4"))
                A["nm"] = tm
                for h in range(8):
                    te = act(lambda e, h=h, u=u: e.activation(
                        PA[:, h, :], S[:, h, :], ACT.Exp, bias=nb4[:, h:h + 1], scale=0.25,
                        accum_out=SU[:, 8 * u + h:8 * u + h + 1]), tm, A.get("aw"), A.get("o1"))
                F[1] = F[2] = te
                A["nb4"] = te
                yield
                s1, s2 = SU[:, 8 * u:8 * u + 8:2], SU[:, 8 * u + 1:8 * u + 8:2]
                tr = dve(lambda e, u=u, s2=s2: e.reciprocal(RS[:, u, :], s2), te)
                dve(lambda e, u=u, s1=s1: e.reciprocal(R1[:, u, :], s1), te)
                tc = dve(lambda e, u=u, s1=s1: e.scalar_tensor_tensor(
                    out=CC[:, u, :], in0=s1, scalar=neglam[:, 0:1], in1=RS[:, u, :], op0=ALU.mult, op1=ALU.mult),
                    tr, t_lam)
                for j in range(4):
                    ta = dve(lambda e, j=j, u=u: e.scalar_tensor_tensor(
                        out=aw[:, j, :], in0=PA[:, 2 * j + 1, :], scalar=CC[:, u, j:j + 1], in1=PA[:, 2 * j, :],
                        op0=ALU.mult, op1=ALU.add), tc, A.get("awf"))
                A["aw"] = ta
                tt = turn(lambda c: aw[:, c, :], 0, ta)
                A["awf"] = tt
                tw = act(lambda e: e.activation(awT[:, :, :], bank(0), ACT.Copy), tt, A.get("pv"))
                F[0] = tw

                def pv(e, u=u):
                    for j in range(4):
                        h = 4 * (2 * (u // 2) + j % 2) + 2 * (u % 2) + j // 2
                        m = e.matmul(bank(0, 32 * j, 32 * j + 32), awT[:, j, :], vA[:, 32 * h:32 * h + 32],
                                     start=True, stop=True)
                    return m
                tp = pe(pv, F[0], tw, t4)
                A["pv"] = tp
                to = dve(lambda e, u=u: e.tensor_tensor(
                    OA[:, 8 * (u // 2):8 * (u // 2) + 8, :]
                    .rearrange("p (i s r) d -> p s r i d", i=2, s=2)[:, u % 2, :, :, :],
                    bank(0, 0, 128).rearrange("p (r i d) -> p r i d", r=2, i=2),
                    R1[:, u, :].rearrange("p (r i) -> p r i", r=2).unsqueeze(3).broadcast_to([128, 2, 2, 32]),
                    ALU.mult), tp, A.get("oa"))
                A["o1"] = to
                F[0] = to
                yield
            t = pool(lambda e: e.tensor_tensor(SQ[:, :, :], OA[:, :, :], OA[:, :, :], ALU.mult), to)
            t = dve(lambda e: e.tensor_reduce(MS[:, :], SQ[:, :, :], AX.X, ALU.add), t)
            t = pool(lambda e: e.tensor_scalar(MS[:, :], MS[:, :], 1.0 / 32, 1e-5, ALU.mult, ALU.add), t)
            t = pool(lambda e: e.tensor_tensor(MR[:, :], MS[:, :], mh[:, :], ALU.pow), t)
            t = pool(lambda e: e.tensor_scalar(MR[:, :], MR[:, :], 1.0 - LAMBDA_INIT, None, ALU.mult), t)
            t = pool(lambda e: e.tensor_tensor(SQ[:, :, :], OA[:, :, :],
                                               MR[:, :].unsqueeze(2).broadcast_to([128, 16, 32]), ALU.mult),
                     t, A.get("sq"))
            A["oa"] = t
            yield
            on = SQ[:, :, :].rearrange("p h d -> p (h d)")
            tt = turn(lambda c: on[:, 128 * c:128 * c + 128], 0, t)
            A["sq"] = tt
            P.base["pool"].append(tt)
            t = act(lambda e: e.activation(oT[:, :, :], bank(0), ACT.Copy), tt, A.get("wo"))
            F[0] = t
            yield

            def wo(e):
                for c in range(4):
                    m = e.matmul(bank(1), oT[:, c, :], WA[:, 3, c, :], start=(c == 0), stop=(c == 3))
                return m
            tp = pe(wo, F[1], t)
            A["wo"] = tp
            t = dve(lambda e: e.tensor_tensor(x, bank(1), x, ALU.add), tp)
            F[1] = t
            x1[b] = t
            yield

        cx = sb(ax, "cx", [128, 2, 512])
        xm = sb(ax, "xm", [128, 512])
        sX = sb(ax, "sX", [128, 2])
        T1 = sb(ax, "T1", [128, 2, 512])
        T2 = sb(ax, "T2", [128, 2, 512])
        kr = sb(ax, "kr", [128, 2, 512])
        qr = sb(ax, "qr", [128, 2, 512])
        kb = sb(ax, "kb", [128, 2, 512], bf16)
        qb = sb(ax, "qb", [128, 2, 512], bf16)
        vh = sb(ax, "vh", [128, 4, 8, 32])
        NM = sb(ax, "NM", [128, 4, 128])
        PX = sb(ax, "PX", [128, 4, 512])
        ox = sb(ax, "ox", [128, 512])
        rc = sb(ax, "rc", [128, 512])
        on2 = sb(ax, "on2", [128, 2, 512])
        x3 = sb(ax, "x3", [128, 512])
        x3T = sb(ax, "x3T", [128, 4, 128])
        t_vh = pool(lambda e: e.memset(vh[:, :, :, :], 0.0))
        t_vh = pool(lambda e: e.memset(vh[:, :, :, 16:17], 1.0), t_vh)
        t_NM = pool(lambda e: e.memset(NM[:, :, :], 0.0))
        NMc = NM[:, :, :].rearrange("p q (j r) -> p q j r", r=32)
        cl = {}
        K = {}

        def load_c(b):
            cl[b] = load(f"d_c{b % 2}", cx[:, b % 2, :], I["ctx"][b, :, :], K.get(("v", b - 2)), K.get(("k", b - 2)))

        pxf = [None] * 4
        pxn = [0]

        def chainX(b):
            x = X[:, b, :]
            c_ = cx[:, b % 2, :]
            t_xm = norm(x, xm[:, :], 1, sX, x1[b], K.get("xm"))
            tk = {}
            for kq in range(2):
                for hh in range(2):
                    b0 = 3 + 2 * hh
                    src = c_ if kq == 0 else xm[:, :]

                    def go(e, kq=kq, hh=hh, b0=b0, src=src):
                        for pm in range(2):
                            m = e.matmul(bank(b0 + pm), WX[:, 4 * kq + 2 * hh + pm, :], src, start=True, stop=True)
                        return m
                    tp = pe(go, F[b0], F[b0 + 1], t_w, cl[b] if kq == 0 else t_xm)
                    if kq == 0:
                        K[("k", b)] = tp
                    else:
                        K["xm"] = tp
                    w = 4 * kq + 2 * hh
                    ta = dve(lambda e, w=w, b0=b0, hh=hh: e.scalar_tensor_tensor(
                        out=T1[:, hh, :], in0=bank(b0), scalar=BX[:, w:w + 1], in1=CST[:, C_COS:C_COS + 512],
                        op0=ALU.add, op1=ALU.mult), tp, K.get(("T", hh)))
                    tb = dve(lambda e, w=w, b0=b0, hh=hh: e.scalar_tensor_tensor(
                        out=T2[:, hh, :], in0=bank(b0 + 1), scalar=BX[:, w + 1:w + 2],
                        in1=CST[:, C_SIN:C_SIN + 512], op0=ALU.add, op1=ALU.mult), tp)
                    F[b0] = ta
                    F[b0 + 1] = tb
                    dst, dsb = (kr, kb) if kq == 0 else (qr, qb)
                    t = pool(lambda e, dst=dst, hh=hh: e.tensor_tensor(
                        dst[:, hh, :], T1[:, hh, :], T2[:, hh, :], ALU.add), tb, K.get(("st", hh)))
                    K[("T", hh)] = t
                    tk[kq, hh] = act(lambda e, dst=dst, dsb=dsb, hh=hh: e.activation(
                        dsb[:, hh, :], dst[:, hh, :], ACT.Copy), t, K.get(("mx", hh)))
                    yield
            for s2 in range(2):
                def go(e, s2=s2):
                    for i in range(2):
                        sc = 2 * s2 + i
                        m = e.matmul(bank(7, 256 * i, 256 * i + 256), c_[:, 128 * sc:128 * sc + 128], WV[:, :],
                                     start=True, stop=True)
                    return m
                tp = pe(go, F[7], cl[b])
                K[("v", b)] = tp
                t_v = act(lambda e, s2=s2: e.activation(
                    vh[:, 2 * s2:2 * s2 + 2, :, 0:16].rearrange("p s h d -> p (s h) d"),
                    bank(7).rearrange("p (s h) -> p s h", h=32)[:, :, 0:16],
                    ACT.Copy), tp, t_vh, K.get("pv"))
                F[7] = t_v
            yield

            def maxes(hh):
                for j in range(4):
                    for qc in range(4):
                        bk = 3 + qc % 2
                        tp = pe(lambda e, j=j, qc=qc, bk=bk: e.matmul(
                            bank(bk), qb[32 * j:32 * j + 32, hh, 128 * qc:128 * qc + 128],
                            kb[32 * j:32 * j + 32, hh, :], start=True, stop=True), F[bk], tk[0, hh], tk[1, hh])
                        tm = dve(lambda e, j=j, qc=qc, bk=bk: e.tensor_reduce(
                            NMc[:, qc, j, 16:17], bank(bk), AX.X, ALU.max, negate=True), tp, t_NM, K.get("nmt"))
                        F[bk] = tm
                    yield
                K[("mx", hh)] = tp
                tt = turn(lambda c: NM[:, c, :], 3, tm)
                K["nmt"] = tt
                t = dve(lambda e: e.tensor_tensor(qr[:, hh, :], bank(3), qr[:, hh, :], ALU.add), tt, tk[1, hh])
                F[3] = t
                K[("qh", hh)] = t
                yield

            def attend(hh):
                for sc in range(4):
                    for j in range(4):
                        bk = 5 + j % 2
                        sl = pxn[0] % 4
                        pxn[0] += 1
                        tp = pe(lambda e, j=j, sc=sc, bk=bk: e.matmul(
                            bank(bk), kr[32 * j:32 * j + 32, hh, 128 * sc:128 * sc + 128],
                            qr[32 * j:32 * j + 32, hh, :], start=True, stop=True), F[bk], K[("qh", hh)])
                        K[("st", hh)] = tp
                        te = act(lambda e, bk=bk, sl=sl: e.activation(
                            PX[:, sl, :], bank(bk), ACT.Exp, scale=0.25), tp, pxf[sl])
                        F[bk] = te
                        later.append((sc, j, sl, te))
                        if len(later) > 2:
                            apply(hh)
                    yield
                while later:
                    apply(hh)
                t_o = act(lambda e: e.activation(ox[:, :], bank(7), ACT.Copy), K["pv"], K.get("ox"))
                F[7] = t_o
                yield
                tb = pe(lambda e: e.matmul(bank(4), CST[:, C_SEL:C_SEL + 128], ox[:, :], start=True, stop=True),
                        F[4], t_o)
                t = dve(lambda e: e.reciprocal(rc[:, :], bank(4)), tb, K.get("rc"))
                F[4] = t
                t = pool(lambda e: e.tensor_tensor(on2[:, hh, :], ox[:, :], rc[:, :], ALU.mult),
                         t, K.get("wo"))
                K["ox"] = K["rc"] = t
                K[("on", hh)] = pool(lambda e: e.tensor_scalar(on2[:, hh, :], on2[:, hh, :], BX[:, 8 + hh:9 + hh],
                                                               None, ALU.add), t)

            later = []

            def apply(hh):
                sc, j, sl, te = later.pop(0)
                K["pv"] = pe(lambda e: e.matmul(
                    ps[32 * j:32 * j + 32, 7 * 512:8 * 512], vh[:, sc, 4 * hh + j, :], PX[:, sl, :],
                    start=(sc == 0), stop=(sc == 3), tile_position=(0, 32 * j)), te, F[7] if sc == 0 else None)
                pxf[sl] = K["pv"]

            yield from maxes(0)
            yield from maxes(1)
            yield from attend(0)
            yield from attend(1)
            yield

            def wo(e):
                for hh in range(2):
                    m = e.matmul(bank(3), WO[:, hh, :], on2[:, hh, :], start=(hh == 0), stop=(hh == 1))
                return m
            tp = pe(wo, F[3], K[("on", 0)], K[("on", 1)])
            K["wo"] = tp
            t = dve(lambda e: e.scalar_tensor_tensor(out=x, in0=bank(3), scalar=BX[:, 10:11], in1=x,
                                                     op0=ALU.add, op1=ALU.add), tp)
            F[3] = t
            x2[b] = t
            yield
            t = norm(x, x3[:, :], 1, ST3[:, b, :], t, K.get("x3"))
            tt = turn(lambda c: x3[:, c:512:4], 3, t)
            K["x3"] = tt
            t = act(lambda e: e.activation(x3T[:, :, :], bank(3), ACT.Copy), tt, K.get("x3T"))
            F[3] = t

            def gate(e):
                for c in range(4):
                    m = e.matmul(bank(4, 0, 32), x3T[:, c, :], GW[:, c, :], start=(c == 0), stop=(c == 3))
                return m
            tp = pe(gate, F[4], t)
            K["x3T"] = tp
            t = dve(lambda e: e.tensor_copy(LG[:, b, :], bank(4, 0, 32)), tp)
            F[4] = t
            yield

        def drain(g):
            for _ in g:
                pass

        for b in range(4):
            load_x(b)
        load_c(0)
        load_c(1)
        drain(chainA(0))
        for b in range(NB):
            gx = chainX(b)
            ga = chainA(b + 1) if b + 1 < NB else iter(())
            live = [gx, ga]
            while live:
                for g in list(live):
                    try:
                        next(g)
                    except StopIteration:
                        live.remove(g)
            if b + 4 < NB:
                load_x(b + 4)
            if b + 2 < NB:
                load_c(b + 2)
            for z in range(4 * b, min(4 * b + 4, NBLK)):
                t_zero = load("d_z", zrows[z, :, :], zt[:, :], t_z)

        P.fence(*P.last("pe", "act", "dve", "pool", "d_z", "d_cst"))
        ax.close()

        mo = ExitStack()
        rt = ExitStack()
        SI = sb(top, "SI", [128, NB, 8], i32)
        W6 = sb(top, "W6", [128, NB, 8])
        EB = sb(top, "EB", [1, NBLK], i32)
        SW = sb(top, "SW", [128, 2, 4, 704])
        SD = sb(top, "SD", [128, 6, 512])
        for n, w in enumerate(("sw_gate", "sw_up")):
            load("d_s", SW[:, n, :, :], I[w].rearrange("(p c) n -> p c n", c=4))
        for s in range(2):
            load("d_s", SD[:, 3 * s:3 * s + 2, :],
                 I["sw_down"][352 * s:352 * s + 256, :].rearrange("(c p) n -> p c n", p=128))
            t_sw = load("d_s", SD[0:96, 3 * s + 2, :], I["sw_down"][352 * s + 256:352 * s + 352, :])

        G = sb(rt, "G", [128, NB, 10])
        G2 = sb(rt, "G2", [128, NB, 10])
        m8 = sb(rt, "m8", [128, NB, 8])
        KP = sb(rt, "KP", [128, NB, 4])
        LM = sb(rt, "LM", [128, NB, 34])
        LM2 = sb(rt, "LM2", [128, NB, 34])
        M = sb(rt, "M", [128, NB, 32])
        RM = sb(rt, "RM", [128, NB + 1, 32])
        SG = sb(rt, "SG", [128, NB, 32])
        SM = sb(rt, "SM", [128, NB])
        SV = sb(rt, "SV", [128, NB, 32])
        S8 = sb(rt, "S8", [128, NB, 8])
        junk = sb(rt, "junk", [128, 2, 32])
        ci = sb(rt, "ci", [128, 32], i32)
        nbf = sb(rt, "nbf", [128, 32])
        cu = sb(rt, "cu", [128, 2, 32])
        bs = sb(rt, "bs", [128, 32])
        E3 = sb(rt, "E3", [1, NBLK, 32])
        E1 = sb(rt, "E1", [1, NBLK])

        def step(fn, t, *a):
            return dve(fn, t, *a)

        te = act(lambda e: e.activation(SG[:, :, :], LG[:, :, :], ACT.Exp, scale=-1.0))
        t = dve(lambda e: e.memset(G[:, :, :], BIG))
        dve(lambda e: e.memset(LM[:, :, :], BIG))
        t = step(lambda e: e.memset(RM[:, :, :], 0.0), t)
        t = step(lambda e: e.tensor_reduce(G[:, :, 0:4], LG[:, :, :].rearrange("p t (g k) -> p t g k", k=8),
                                           AX.X, ALU.max), t)
        for n in range(NB):
            t = step(lambda e, n=n: e.max(m8[:, n, :], G[:, n, :]), t)
        for n in range(NB):
            t = step(lambda e, n=n: e.match_replace(G2[:, n, :], m8[:, n, :], G[:, n, :], -BIG), t)
        t = step(lambda e: e.tensor_scalar(KP[:, :, :], G2[:, :, 0:4], -BIG, None, ALU.is_equal), t)
        t = step(lambda e: e.tensor_scalar(KP[:, :, :], KP[:, :, :], -1.0, 1e30, ALU.add, ALU.mult), t)
        t = step(lambda e: e.tensor_tensor(
            LM[:, :, 0:32].rearrange("p t (g k) -> p t g k", k=8), LG[:, :, :].rearrange("p t (g k) -> p t g k", k=8),
            KP[:, :, :].unsqueeze(3).broadcast_to([128, NB, 4, 8]), ALU.add), t)
        for n in range(NB):
            t = step(lambda e, n=n: e.max(m8[:, n, :], LM[:, n, :]), t)
        for n in range(NB):
            t = step(lambda e, n=n: e.match_replace(LM2[:, n, :], m8[:, n, :], LM[:, n, :], -BIG), t)
        t = step(lambda e: e.tensor_scalar(M[:, :, :], LM2[:, :, 0:32], -BIG, None, ALU.is_equal), t)
        for n in range(NB):
            t = step(lambda e, n=n: e.tensor_tensor(RM[:, n + 1, :], RM[:, n, :], M[:, n, :], ALU.add), t)

        def ranks(e):
            for h in range(2):
                e.matmul(bank(h), CST[:, C_TRI:C_TRI + 128], M[:, 16 * h:16 * h + 16, :], start=True, stop=False)
                e.matmul(bank(h), CST[:, C_ONE:C_ONE + 128], RM[:, 16 * h:16 * h + 16, :], start=False, stop=True)
            return e.matmul(bank(2, 0, 32), CST[:, C_ONE:C_ONE + 128], RM[:, NB, :], start=True, stop=True)
        tr = pe(ranks, t)
        t = step(lambda e: e.tensor_scalar(SG[:, :, :], SG[:, :, :], 1.0, None, ALU.add), t, te)
        t = step(lambda e: e.reciprocal(SG[:, :, :], SG[:, :, :]), t)
        t = step(lambda e: e.tensor_tensor(SG[:, :, :], SG[:, :, :], M[:, :, :], ALU.mult), t)
        t = step(lambda e: e.tensor_reduce(SM[:, :], SG[:, :, :], AX.X, ALU.add), t)
        t = step(lambda e: e.reciprocal(SM[:, :], SM[:, :]), t)
        t = step(lambda e: e.tensor_tensor(SG[:, :, :], SG[:, :, :], SM[:, :].unsqueeze(2).broadcast_to([128, NB, 32]),
                                           ALU.mult), t)
        t = step(lambda e: e.tensor_scalar(ci[:, :], bank(2, 0, 32), float(BLK - 1), None, ALU.add), t, tr)
        t = step(lambda e: e.tensor_scalar(ci[:, :], ci[:, :], 8, None, ALU.logical_shift_right), t)
        t = step(lambda e: e.tensor_copy(nbf[:, :], ci[:, :]), t)
        t = step(lambda e: e.tensor_copy(cu[:, 0, :], nbf[:, :]), t)
        for k in range(5):
            s, a, b_ = 1 << k, k % 2, 1 - k % 2
            dve(lambda e, s=s, a=a, b_=b_: e.tensor_copy(cu[:, b_, 0:s], cu[:, a, 0:s]), t)
            t = step(lambda e, s=s, a=a, b_=b_: e.tensor_tensor(cu[:, b_, s:32], cu[:, a, s:32], cu[:, a, 0:32 - s],
                                                                ALU.add), t)
        t = step(lambda e: e.tensor_tensor(bs[:, :], cu[:, 1, :], nbf[:, :], ALU.subtract), t)
        t = step(lambda e: e.tensor_scalar(bs[:, :], bs[:, :], float(BLK), 1.0, ALU.mult, ALU.add), t)
        for h in range(2):
            t = step(lambda e, h=h: e.tensor_tensor(
                SV[:, 16 * h:16 * h + 16, :], bank(h).rearrange("p (t k) -> p t k", k=32),
                bs[:, :].unsqueeze(1).broadcast_to([128, 16, 32]), ALU.add), t)
        t = step(lambda e: e.tensor_tensor(SV[:, :, :], SV[:, :, :], M[:, :, :], ALU.mult), t)
        for n in range(NB):
            t = step(lambda e, n=n: e.max(S8[:, n, :], SV[:, n, :]), t)
        t_si = t = step(lambda e: e.tensor_scalar(SI[:, :, :], S8[:, :, :], -1.0, None, ALU.add), t)
        t = step(lambda e: e.tensor_tensor(
            E3[:, :, :], cu[0:1, 1, :].unsqueeze(1).broadcast_to([1, NBLK, 32]),
            CST[0:1, C_BI:C_BI + NBLK].unsqueeze(2).broadcast_to([1, NBLK, 32]), ALU.is_le), t)
        t = step(lambda e: e.tensor_reduce(E1[:, :], E3[:, :, :], AX.X, ALU.add), t)
        t_eb = t = step(lambda e: e.tensor_scalar(EB[:, :], E1[:, :], 31.0, None, ALU.min), t)
        jt = [None, None]
        for n in range(NB):
            for k in range(6):
                q = k % 2
                jt[q] = dve(lambda e, n=n, k=k, q=q: e.scalar_tensor_tensor(
                    out=junk[:, q, :], in0=SV[:, n, :], scalar=S8[:, n, k:k + 1], in1=SG[:, n, :],
                    op0=ALU.is_equal, op1=ALU.mult, accum_out=W6[:, n, k:k + 1]), t, jt[q])
        t_w6 = dve(lambda e: e.memset(NR3[:, :], 0.0), jt[0], jt[1])
        P.fence(t_w6, *P.last("pe", "act", "pool"))
        rt.close()

        WG = sb(mo, "WG", [128, 2, 2, 4, 352])
        WD = sb(mo, "WD", [128, 2, 3, 512])
        NX = 4
        XI = sb(mo, "XI", [128, NX, 512])
        XT = sb(mo, "XT", [128, 2, 4, 128])
        HS = sb(mo, "HS", [128, 2, 352])
        HT = sb(mo, "HT", [128, 2, 3, 128])
        YO = sb(mo, "YO", [128, 4, 512])
        xif, xtf, yof = [None] * NX, [None] * 2, [None] * 4
        wfree, hsf, htf = [None, None], [None, None], [None, None]
        scat = []
        items = [("s", n, s) for n in range(NB) for s in range(2)] + \
                [("m", b, i) for b in range(NBLK) for i in range(2)]
        N = len(items)
        tin, txT, twt, th, tht = {}, {}, {}, {}, {}
        src = {}
        xr = [0]
        prev_s = [[] for _ in range(NX)]

        def fetch(n):
            kind, a, i = items[n]
            if kind == "s" and i == 1:
                return
            sl = xr[0] % NX
            xr[0] += 1
            src[n] = sl
            if kind == "s":
                t = pool(lambda e: e.tensor_scalar(XI[:, sl, :], X[:, a, :], ST3[:, a, 0:1], ST3[:, a, 1:2],
                                                   ALU.subtract, ALU.mult), xif[sl], *prev_s[sl])
                prev_s[sl] = []
                for k in range(6):
                    ts = P.put("pool", lambda e, k=k: e.indirect_dma_start(
                        out=XS[:, :], out_offset=bass.IndirectOffsetOnAxis(ap=SI[:, a, k:k + 1], axis=0),
                        in_=XI[:, sl, :], in_offset=None), t, t_si, sem=f"d_sc{sl}", by=16)
                prev_s[sl] = [ts]
                tin[n] = t
            else:
                tin[n] = load(f"d_xi{sl}", XI[:, sl, :], XS[BLK * a + 128 * i:BLK * a + 128 * i + 128, :],
                              xif[sl], *P.last(*[f"d_sc{q}" for q in range(NX)]))

        def weights(b):
            q = b % 2

            def go(e, w=0):
                r = regs.setdefault(b, e.value_load(EB[0:1, b:b + 1], min_val=0, max_val=31)) if w == 0 else regs[b]
                if w == 2:
                    return e.dma_start(WD[:, q, 0:2, :], I["w_down"][bass.ds(r, 1), 0:256, :]
                                       .rearrange("a (c p) n -> p (a c) n", p=128))
                if w == 3:
                    return e.dma_start(WD[0:96, q, 2, :], I["w_down"][bass.ds(r, 1), 256:352, :]
                                       .rearrange("a p n -> p (a n)"))
                return e.dma_start(WG[:, q, w, :, :], I["w_gate" if w == 0 else "w_up"][bass.ds(r, 1), :, :]
                                   .rearrange("a (p c) n -> p (a c) n", c=4))
            for w in range(4):
                twt[b] = P.put("sp", lambda e, w=w: go(e, w), t_eb, wfree[q], sem=f"d_wt{q}", by=16)

        regs = {}

        def s1(n):
            kind, a, i = items[n]
            if kind == "s" and i == 1:
                txT[n] = txT[n - 1]
                src[n] = src[n - 1]
                xq[n] = xq[n - 1]
                return
            q = xc[0] % 2
            xc[0] += 1
            xq[n] = q
            sl = src[n]

            def go(e):
                for c in range(4):
                    m = e.transpose(bank(q, 128 * c, 128 * c + 128), XI[:, sl, c:512:4], ident)
                return m
            tt = pe(go, F[q], tin[n])
            xif[sl] = tt
            txT[n] = act(lambda e: e.activation(XT[:, q, :, :], bank(q), ACT.Copy), tt, xtf[q])
            F[q] = txT[n]

        xq, xc = {}, [0]

        def s2(n):
            kind, a, i = items[n]
            q = n % 2
            bg, bu = 2 + q, 4 + q

            def go(e):
                for c in range(4):
                    for w in range(2):
                        wt = SW[:, w, c, 352 * i:352 * i + 352] if kind == "s" else WG[:, a % 2, w, c, :]
                        m = e.matmul(bank(bg if w == 0 else bu, 0, 352), XT[:, xq[n], c, :], wt,
                                     start=(c == 0), stop=(c == 3))
                return m
            tp = pe(go, F[bg], F[bu], txT[n], t_sw if kind == "s" else twt[a])
            xtf[xq[n]] = tp
            tg = act(lambda e: e.activation(HS[:, q, :], bank(bg, 0, 352), ACT.Silu), tp, hsf[q])
            F[bg] = tg
            th[n] = dve(lambda e: e.tensor_tensor(HS[:, q, :], bank(bu, 0, 352), HS[:, q, :], ALU.mult), tg)
            F[bu] = th[n]

        def s3(n):
            q = n % 2

            def go(e):
                for c in range(3):
                    k = 128 if c < 2 else 96
                    m = e.transpose(ps[0:k, 6 * 512 + 128 * c:6 * 512 + 128 * c + 128],
                                    HS[:, q, 128 * c:128 * c + k], ident)
                return m
            tt = pe(go, F[6], th[n])
            hsf[q] = tt
            dve(lambda e: e.tensor_copy(HT[:, q, 0:2, :], bank(6, 0, 256)), tt, htf[q])
            tht[n] = dve(lambda e: e.tensor_copy(HT[0:96, q, 2, :], ps[0:96, 6 * 512 + 256:6 * 512 + 384]), tt)
            F[6] = tht[n]

        def s4(n):
            kind, a, i = items[n]
            q = n % 2

            def go(e):
                for c in range(3):
                    k = 128 if c < 2 else 96
                    wt = SD[0:k, 3 * i + c, :] if kind == "s" else WD[0:k, a % 2, c, :]
                    first = c == 0 and not (kind == "s" and i == 1)
                    last = c == 2 and not (kind == "s" and i == 0)
                    m = e.matmul(bank(7), HT[0:k, q, c, :], wt, start=first, stop=last)
                return m
            tp = pe(go, F[7] if not (kind == "s" and i == 1) else None, tht[n])
            htf[q] = tp
            if kind == "s":
                if i == 1:
                    F[7] = dve(lambda e: e.tensor_tensor(X[:, a, :], bank(7), X[:, a, :], ALU.add), tp, tin[n - 1])
                return
            if i == 1:
                wfree[a % 2] = tp
                if a + 2 < NBLK:
                    weights(a + 2)
            yq = n % 4
            ev = act if i == 0 else dve
            F[7] = (act(lambda e: e.activation(YO[:, yq, :], bank(7), ACT.Copy), tp, yof[yq]) if i == 0 else
                    dve(lambda e: e.tensor_copy(YO[:, yq, :], bank(7)), tp, yof[yq]))
            r0 = BLK * a + 128 * i
            yof[yq] = P.put("act", lambda e: e.dma_start(YS[r0:r0 + 128, :], YO[:, yq, :]), F[7],
                            sem=f"d_y{yq}", by=16)

        weights(0)
        weights(1)
        nf = 0

        def ahead(n):
            nonlocal nf
            while nf < min(n, N):
                fetch(nf)
                nf += 1
        ahead(2)
        s1(0)
        for n in range(N + 1):
            ahead(n + 4)
            if n + 1 < N:
                s1(n + 1)
            if n >= 1:
                s3(n - 1)
            if n < N:
                s2(n)
            if n >= 1:
                s4(n - 1)

        P.fence(*P.last("pe", "act", "dve", "pool"), *P.last(*[f"d_y{q}" for q in range(4)]))
        mo.close()
        co = ExitStack()
        GB = sb(co, "GB", [128, 12, 512])
        gf = [None] * 12
        g = 0
        for n in range(NB):
            for k in range(6):
                sl = g % 12
                g += 1
                tg = P.put("pool", lambda e, n=n, k=k, sl=sl: e.indirect_dma_start(
                    out=GB[:, sl, :], out_offset=None, in_=YS[:, :],
                    in_offset=bass.IndirectOffsetOnAxis(ap=SI[:, n, k:k + 1], axis=0)),
                    gf[sl], sem=f"d_g{sl}", by=16)
                t = dve(lambda e, n=n, k=k, sl=sl: e.scalar_tensor_tensor(
                    out=X[:, n, :], in0=GB[:, sl, :], scalar=W6[:, n, k:k + 1], in1=X[:, n, :],
                    op0=ALU.mult, op1=ALU.add), tg, t)
                gf[sl] = t
            t_out = P.put("sp", lambda e, n=n: e.dma_start(out[n, :, :], X[:, n, :]), t, sem="d_out", by=16)
        P.quiet("sp", lambda e: e.wait_ge(sems["d_out"], t_out[1]))
        co.close()

        sems = {k: top.enter_context(nc.semaphore("s_" + k)) for k in P.count}
        block = top.enter_context(nc.Block())

        @block.tensor
        def _(e):
            P.emit("pe", e, sems)

        @block.scalar
        def _(e):
            P.emit("act", e, sems)

        @block.vector
        def _(e):
            P.emit("dve", e, sems)

        @block.gpsimd
        def _(e):
            P.emit("pool", e, sems)

        @block.sync
        def _(e):
            P.emit("sp", e, sems)


def constants():
    c = np.zeros((128, C_N), np.float32)
    p = np.arange(128)
    c[:, C_ID:C_ID + 128] = np.eye(128)
    c[:, C_TRI:C_TRI + 128] = p[:, None] < p[None, :]
    c[:, C_ONE:C_ONE + 128] = 1.0
    c[:, C_SEL:C_SEL + 128] = p[:, None] == (p[None, :] // 32) * 32 + 16
    inv = (np.float32(1.0) / np.float32(10000.0) ** (np.arange(0, 16, 2, dtype=np.float32) / np.float32(16))
           ).astype(np.float32)
    pos = (np.arange(512, dtype=np.float32)[:, None] * inv[None, :]).astype(np.float32)
    cos, sin = np.cos(pos).astype(np.float32), np.sin(pos).astype(np.float32)
    for r in range(128):
        d = r % 32
        if d < 16:
            c[r, C_COS:C_COS + 512] = cos[:, d % 8]
            c[r, C_SIN:C_SIN + 512] = -sin[:, d % 8] if d < 8 else sin[:, d % 8]
        elif d == 16:
            c[r, C_COS:C_COS + 512] = 1.0
    c[:, C_MSK:C_MSK + 128] = np.where(p[None, :] > p[:, None], -1e30, 0.0)
    c[:, C_AB] = p % 32 < 16
    c[:, C_AB + 1] = p % 32 >= 16
    c[:, C_BI:C_BI + 128] = p[None, :]
    return c


def laid_out(inputs):
    g = {k: np.asarray(v) for k, v in inputs.items()}
    swap = np.concatenate([np.arange(8, 16), np.arange(0, 8)])
    Wk, Wq = g["L0_xattn_Wk"], g["L0_xattn_Wq"]
    wx = np.zeros((128, 8, 128), np.float32)
    bx = np.zeros((128, 11), np.float32)
    wv = np.zeros((128, 256), np.float32)
    wo = np.zeros((128, 2, 128), np.float32)
    for kq, (W, b) in enumerate(((Wk, g["L0_xattn_bk"]), (Wq, g["L0_xattn_bq"]))):
        for hh in range(2):
            for j in range(4):
                rows = 16 * (4 * hh + j) + np.arange(16)
                for pm, r in enumerate((rows, rows[swap])):
                    wx[:, 4 * kq + 2 * hh + pm, 32 * j:32 * j + 16] = W[r, :].T
                    bx[32 * j:32 * j + 16, 4 * kq + 2 * hh + pm] = b[r]
    for hh in range(2):
        bx[16::32, 2 * hh] = 1.0
        for j in range(4):
            rows = 16 * (4 * hh + j) + np.arange(16)
            wv[:, 128 * hh + 32 * j:128 * hh + 32 * j + 16] = g["L0_xattn_Wv"][rows, :].T
            wo[32 * j:32 * j + 16, hh, :] = g["L0_xattn_Wo"][:, rows].T
            bx[32 * j:32 * j + 16, 8 + hh] = g["L0_xattn_bv"][rows]
    bx[:, 10] = g["L0_xattn_bo"]
    a = {
        "x": g["x"], "ctx": g["ctx_2048"], "cst": constants(), "wx": wx, "wv": wv, "wo": wo, "bx": bx,
        "Wq": g["L0_attn_Wq"], "Wk": g["L0_attn_Wk"], "Wv": g["L0_attn_Wv"], "Wo": g["L0_attn_Wo"],
        "lq": np.stack([g["L0_attn_lq1"], g["L0_attn_lk1"], g["L0_attn_lq2"], g["L0_attn_lk2"]]),
        "gate_w": g["L0_ffn_gate_w"], "w_gate": g["L0_ffn_w_gate"], "w_up": g["L0_ffn_w_up"],
        "w_down": g["L0_ffn_w_down"], "sw_gate": g["L0_ffn_sw_gate"], "sw_up": g["L0_ffn_sw_up"],
        "sw_down": g["L0_ffn_sw_down"],
    }
    return {k: np.ascontiguousarray(v) for k, v in a.items()}


def kernel(**inputs):
    import concourse.bacc as bacc
    from concourse.bass_utils import run_bass_kernel_spmd

    nc = bacc.Bacc("TRN2", target_bir_lowering=False, num_devices=1)
    arrays, aps = {}, {}
    for name, a in laid_out(inputs).items():
        arrays[f"in_{name}"] = a
        aps[name] = nc.dram_tensor(f"in_{name}", a.shape, mybir.dt.from_np(a.dtype), kind="ExternalInput").ap()
    out = nc.dram_tensor("out_0", (NB, 128, 512), mybir.dt.float32, kind="ExternalOutput").ap()
    build(nc, aps, out)
    r = run_bass_kernel_spmd(nc, [arrays], core_ids=[0])
    return r.results[0]["out_0"]
```

```python
import math
import numpy as np
import concourse.bass as bass
from concourse import mybir
from contextlib import ExitStack

NB = 32
BLK = 256
NBLK = 127
NSLOT = NBLK * BLK
LAMBDA_INIT = 0.8 - 0.6 * math.exp(-0.3 * 12)
BIG = 3.0e38
C_ID, C_TRI, C_ONE, C_SEL, C_COS, C_SIN, C_MSK, C_AB, C_BI = 0, 128, 256, 384, 512, 1024, 1536, 1664, 1667
C_N = C_BI + 128
SPREAD = (0, 0, 1, 1, 0, 0, 1, 0, 1, 0)
W_KHI, W_KLO, W_QHI, W_QLO = 6, 5, 2, 0
NXB = 6
AS = 17
PRE = 16


class Plan:

    def __init__(self):
        self.lists = {n: [] for n in ("pe", "act", "dve", "pool", "sp")}
        self.count = {}
        self.base = {n: [] for n in self.lists}

    def put(self, eng, fn, *after, sem=None, by=1):
        key = sem or eng
        self.count[key] = self.count.get(key, 0) + by
        self.lists[eng].append((self.base[eng] + list(after), fn, key, by))
        self.base[eng] = []
        return (key, self.count[key])

    def quiet(self, eng, fn, *after):
        self.lists[eng].append((self.base[eng] + list(after), fn, None, 0))
        self.base[eng] = []

    def fence(self, *tokens):
        for n in self.base:
            self.base[n] = list(tokens)

    def last(self, *keys):
        return [(k, self.count[k]) for k in keys if self.count.get(k)]

    def emit(self, name, eng, sems):
        seen = {}
        for after, fn, key, by in self.lists[name]:
            for t in after:
                if t is not None and seen.get(t[0], 0) < t[1]:
                    eng.wait_ge(sems[t[0]], t[1])
                    seen[t[0]] = t[1]
            ins = fn(eng)
            if key:
                ins.then_inc(sems[key], by)


def build(nc, I, out):
    f32, f32r, bf16, i32 = mybir.dt.float32, mybir.dt.float32r, mybir.dt.bfloat16, mybir.dt.int32
    ALU, ACT, AX = mybir.AluOpType, mybir.ActivationFunctionType, mybir.AxisListType
    P = Plan()

    def pe(fn, *a): return P.put("pe", fn, *a)
    def act(fn, *a): return P.put("act", fn, *a)
    def dve(fn, *a): return P.put("dve", fn, *a)
    def pool(fn, *a): return P.put("pool", fn, *a)
    def load(sem, dst, src, *a, eng="sp"):
        return P.put(eng, lambda e: e.dma_start(dst, src), *a, sem=sem, by=16)

    top = ExitStack()
    with top:
        def sb(stack, name, shape, dt=f32):
            return stack.enter_context(nc.sbuf_tensor(name, shape, dt))

        XS = nc.dram_tensor("xs_sorted", (NSLOT, 512), f32, kind="Internal").ap()
        YS = nc.dram_tensor("ys_sorted", (NSLOT, 512), f32, kind="Internal").ap()

        ps = top.enter_context(nc.psum_tensor("ps", [128, 8 * 512], f32))

        def bank(i, a=0, b=512):
            return ps[:, i * 512 + a:i * 512 + b]

        XD = nc.dram_tensor("x_after", (NB, 128, 512), f32, kind="Internal").ap()
        YD = nc.dram_tensor("x_shared", (NB, 128, 512), f32, kind="Internal").ap()
        CST = sb(top, "CST", [128, C_N])
        ident = CST[:, C_ID:C_ID + 128]
        LG = sb(top, "LG", [128, NB, 32])
        ST3 = sb(top, "ST3", [128, NB, 2])
        F = [None] * 8

        t_cst = load("d_cst", CST[:, :], I["cst"])
        mh = sb(top, "mh", [128, 16])
        t_mh = pool(lambda e: e.memset(mh[:, :], -0.5))

        ax = ExitStack()
        XB = sb(ax, "XB", [128, NXB, 512])
        WA = sb(ax, "WA", [128, 4, 4, 512])
        WX = sb(ax, "WX", [128, 4, 128])
        WV = sb(ax, "WV", [128, 256])
        WO = sb(ax, "WO", [128, 2, 128])
        BX = sb(ax, "BX", [128, 7])
        GW = sb(ax, "GW", [128, 4, 32])
        LQ = sb(ax, "LQ", [128, 4, 16])
        idb = sb(ax, "idb", [128, 128], bf16)
        mkb = sb(ax, "mkb", [128, 4, 128], bf16)
        zt = sb(ax, "zt", [128, 512])
        REP = sb(ax, "REP", [128, 8, 320], f32r)
        KS = sb(ax, "KS", [128, 8, 512], f32r)
        QS = sb(ax, "QS", [128, 8, 512], f32r)
        for n, w in enumerate(("Wq", "Wk", "Wv", "Wo")):
            load("d_w", WA[:, n, :, :], I[w].rearrange("(c p) n -> p c n", p=128))
        load("d_w", WX[:, :, :], I["wx"])
        load("d_w", WV[:, :], I["wv"])
        load("d_w", WO[:, :, :], I["wo"])
        load("d_w", BX[:, :], I["bx"])
        load("d_w", GW[:, :, :], I["gate_w"].rearrange("(p c) n -> p c n", c=4))
        t_w = load("d_w", LQ[:, :, :], I["lq"].partition_broadcast(128))

        t_idb = dve(lambda e: e.tensor_copy(idb[:, :], ident), t_cst)
        t_mkb = dve(lambda e: e.tensor_copy(
            mkb[:, :, :], CST[:, C_MSK:C_MSK + 128].unsqueeze(1).broadcast_to([128, 4, 128])), t_cst)
        PX = sb(ax, "PX", [128, 4, 512])
        RT = PX[:, 0:2, :]
        t_rep = []
        for h in range(8):
            q = h % 2
            t = load(f"d_rt{q}", RT[:, q, 0:320], I["rep"][:, h, :], t_rep[h - 2] if h >= 2 else None)
            t_rep.append(dve(lambda e, h=h, q=q: e.tensor_copy(REP[:, h, :], RT[:, q, 0:320]), t))
        t_rep = t_rep[-1]
        lm = sb(ax, "lm", [128, 2, 16])
        ls = sb(ax, "ls", [128, 2])
        le = sb(ax, "le", [128, 2])
        neglam = sb(ax, "neglam", [128, 1])
        t = dve(lambda e: e.tensor_tensor(lm[:, :, :], LQ[:, 0:4:2, :], LQ[:, 1:4:2, :], ALU.mult), t_w)
        t = dve(lambda e: e.tensor_reduce(ls[:, :], lm[:, :, :], AX.X, ALU.add), t)
        t = act(lambda e: e.activation(le[:, :], ls[:, :], ACT.Exp), t)
        t = dve(lambda e: e.tensor_tensor(neglam[:, :], le[:, 1:2], le[:, 0:1], ALU.subtract), t)
        t_lam = dve(lambda e: e.tensor_scalar(neglam[:, :], neglam[:, :], -LAMBDA_INIT, None, ALU.add), t)

        t_z = pool(lambda e: e.memset(zt[:, :], 0.0))
        zrows = XS.rearrange("(n p) d -> n p d", p=128)

        st6 = sb(ax, "st6", [128, 2, 6])
        mv = sb(ax, "mv", [128, 2, 2])
        ve = sb(ax, "ve", [128, 2, 1])
        lnfree = [None, None]

        def norm(x, dst, which, stats, *after):
            s, m, v = st6[:, which, :], mv[:, which, :], ve[:, which, :]
            t = dve(lambda e: e.bn_stats(s, x), *after, lnfree[which])
            t = dve(lambda e: e.bn_aggr(m, s), t)
            t = pool(lambda e: e.tensor_scalar(v, m[:, 1:2], 1e-5, None, ALU.add), t, t_mh)
            t = pool(lambda e: e.tensor_tensor(stats[:, 1:2], v, mh[:, 0:1], ALU.pow), t)
            t = pool(lambda e: e.tensor_copy(stats[:, 0:1], m[:, 0:1]), t)
            yield
            yield
            lnfree[which] = t = dve(lambda e: e.tensor_scalar(dst, x, stats[:, 0:1], stats[:, 1:2],
                                                              ALU.subtract, ALU.mult), t)
            return t

        def turn(src, b, *after):
            def go(e):
                for c in range(4):
                    m = e.transpose(bank(b, 128 * c, 128 * c + 128), src(c), ident)
                return m
            return pe(go, F[b], *after, t_cst)

        xn = sb(ax, "xn", [128, 512])
        sA = sb(ax, "sA", [128, 2])
        xT = sb(ax, "xT", [128, 4, 128])
        qA = sb(ax, "qA", [128, 4, 128])
        qB = sb(ax, "qB", [128, 4, 128])
        kT = sb(ax, "kT", [128, 4, 128])
        vA = sb(ax, "vA", [128, 512])
        nm = sb(ax, "nm", [128, 8])
        nb4 = sb(ax, "nb4", [128, 8])
        PA = sb(ax, "PA", [128, 8, 128])
        SU = sb(ax, "SU", [128, 32])
        RS = sb(ax, "RS", [128, 4, 4])
        CC = sb(ax, "CC", [128, 4, 4])
        aw = sb(ax, "aw", [128, 4, 128])
        awT = sb(ax, "awT", [128, 4, 128])
        R1 = sb(ax, "R1", [128, 4, 4])
        OA = sb(ax, "OA", [128, 16, 32])
        SQ = sb(ax, "SQ", [128, 16, 32])
        MS = sb(ax, "MS", [128, 16])
        MR = sb(ax, "MR", [128, 16])
        oT = sb(ax, "oT", [128, 4, 128])
        xl = {}
        x1 = {}
        x2, xs = {}, {}
        A = {}

        def load_x(b):
            xl[b] = load(f"d_x{b % NXB}", XB[:, b % NXB, :], I["x"][b, :, :], x2.get(b - NXB), xs.get(b - NXB))

        def chainA(b):
            x = XB[:, b % NXB, :]
            t_xn = yield from norm(x, xn[:, :], 0, sA, xl[b], A.get("xn"))
            yield
            A["xn"] = tt = turn(lambda c: xn[:, 128 * c:128 * c + 128], 0, t_xn)
            F[0] = t_xT = act(lambda e: e.activation(xT[:, :, :], bank(0), ACT.Copy), tt, A.get("xT"))
            yield
            yield

            def proj(b_, w):
                def go(e):
                    for ct in range(4):
                        for c in range(4):
                            m = e.matmul(bank(b_, 128 * ct, 128 * ct + 128),
                                         WA[:, w, c, 128 * ct:128 * ct + 128], xT[:, c, :],
                                         start=(c == 0), stop=(c == 3))
                    return m
                return pe(go, F[b_], t_xT, t_w)

            tq = proj(1, 0)
            yield
            t1 = act(lambda e: e.activation(qA[:, :, :], bank(1), ACT.Copy, scale=CST[:, C_AB:C_AB + 1]),
                     tq, A.get("s"))
            tk = proj(2, 1)
            yield
            F[1] = t2 = dve(lambda e: e.tensor_scalar(qB[:, :, :], bank(1), CST[:, C_AB + 1:C_AB + 2], None,
                                                      ALU.mult), tq, t1, A.get("s"))
            F[2] = t3 = act(lambda e: e.activation(kT[:, :, :], bank(2), ACT.Copy), tk, A.get("s"))

            def values(e):
                for c in range(4):
                    m = e.matmul(bank(0), xT[:, c, :], WA[:, 2, c, :], start=(c == 0), stop=(c == 3))
                return m
            A["xT"] = tv = pe(values, F[0], t_xT)
            yield
            F[0] = t4 = act(lambda e: e.activation(vA[:, :], bank(0), ACT.Copy), tv, A.get("pv"))
            S = ps[:, 512:1536].rearrange("p (h k) -> p h k", k=128)
            done = {}

            def scores(u):
                def sc(e):
                    for r in range(2):
                        e.matmul(bank(1 + r), idb[:, :], mkb[:, :, :], start=True, stop=False,
                                 skip_group_check=True)
                    for i in range(2):
                        for hf in range(2):
                            for r in range(2):
                                q, j, ct = (qB if hf else qA), 2 * (u % 2) + r, 2 * (u // 2) + i
                                col = i * 256 + hf * 128
                                m = e.matmul(bank(1 + r, col, col + 128), q[32 * j:32 * j + 32, ct, :],
                                             kT[32 * j:32 * j + 32, ct, :], start=False,
                                             stop=i == 1 and hf == 1, skip_group_check=True)
                    return m
                A["s"] = pe(sc, F[1], F[2], t1, t2, t3, t_idb, t_mkb)

            def tops(u):
                A["nm"] = tm = dve(lambda e: e.tensor_reduce(nm[:, :], S, AX.X, ALU.max, negate=True),
                                   A["s"], A.get("nm"))
                A["nm"] = done["m", u] = dve(lambda e: e.tensor_scalar(nb4[:, :], nm[:, :], 0.25, None, ALU.mult),
                                             tm, A.get("nb4"))

            def exps(u, part):
                for h in range(4 * part, 4 * part + 4):
                    te = act(lambda e, h=h: e.activation(
                        PA[:, h, :], S[:, h, :], ACT.Exp, bias=nb4[:, h:h + 1], scale=0.25,
                        accum_out=SU[:, 8 * u + h:8 * u + h + 1]), done["m", u], A.get("aw"), A.get("o1"))
                F[1] = F[2] = A["nb4"] = done["e", u] = te

            def weigh(u):
                te = done["e", u]
                s1, s2 = SU[:, 8 * u:8 * u + 8:2], SU[:, 8 * u + 1:8 * u + 8:2]
                tr = dve(lambda e: e.reciprocal(RS[:, u, :], s2), te)
                done["r", u] = dve(lambda e: e.reciprocal(R1[:, u, :], s1), te, A.get("oa"))
                tc = dve(lambda e: e.scalar_tensor_tensor(
                    out=CC[:, u, :], in0=s1, scalar=neglam[:, 0:1], in1=RS[:, u, :], op0=ALU.mult, op1=ALU.mult),
                    tr, t_lam)
                for j in range(4):
                    ta = dve(lambda e, j=j: e.scalar_tensor_tensor(
                        out=aw[:, j, :], in0=PA[:, 2 * j + 1, :], scalar=CC[:, u, j:j + 1], in1=PA[:, 2 * j, :],
                        op0=ALU.mult, op1=ALU.add), tc, A.get("awf"))
                A["aw"] = ta

            def turned(u):
                A["awf"] = tt = turn(lambda c: aw[:, c, :], 0, A["aw"])
                F[0] = done["t", u] = act(lambda e: e.activation(awT[:, :, :], bank(0), ACT.Copy), tt, A.get("pv"))

            def values_of(u):
                def pv(e):
                    for j in range(4):
                        h = 4 * (2 * (u // 2) + j % 2) + 2 * (u % 2) + j // 2
                        m = e.matmul(bank(0, 32 * j, 32 * j + 32), awT[:, j, :], vA[:, 32 * h:32 * h + 32],
                                     start=True, stop=True)
                    return m
                A["pv"] = pe(pv, F[0], done["t", u], t4)

            def scaled(u):
                F[0] = A["o1"] = done["o", u] = dve(lambda e: e.tensor_tensor(
                    OA[:, 8 * (u // 2):8 * (u // 2) + 8, :]
                    .rearrange("p (i s r) d -> p s r i d", i=2, s=2)[:, u % 2, :, :, :],
                    bank(0, 0, 128).rearrange("p (r i d) -> p r i d", r=2, i=2),
                    R1[:, u, :].rearrange("p (r i) -> p r i", r=2).unsqueeze(3).broadcast_to([128, 2, 2, 32]),
                    ALU.mult), A["pv"], done["r", u], A.get("oa"))

            scores(0)
            yield
            tops(0)
            yield
            exps(0, 0)
            yield
            exps(0, 1)
            yield
            for u in range(4):
                if u:
                    scaled(u - 1)
                weigh(u)
                if u < 3:
                    scores(u + 1)
                yield
                turned(u)
                if u < 3:
                    tops(u + 1)
                yield
                if u < 3:
                    exps(u + 1, 0)
                yield
                values_of(u)
                if u < 3:
                    exps(u + 1, 1)
                    yield
            scaled(3)
            to = done["o", 3]
            t = act(lambda e: e.activation(SQ[:, :, :], OA[:, :, :], ACT.Square), to, A.get("sq"))
            yield
            t = dve(lambda e: e.tensor_reduce(MS[:, :], SQ[:, :, :], AX.X, ALU.add), t)
            t = pool(lambda e: e.tensor_scalar(MS[:, :], MS[:, :], 1.0 / 32, 1e-5, ALU.mult, ALU.add), t)
            t = pool(lambda e: e.tensor_tensor(MR[:, :], MS[:, :], mh[:, :], ALU.pow), t)
            t = pool(lambda e: e.tensor_scalar(MR[:, :], MR[:, :], 1.0 - LAMBDA_INIT, None, ALU.mult), t)
            yield
            yield
            yield
            A["oa"] = t = dve(lambda e: e.tensor_tensor(
                SQ[:, :, :], OA[:, :, :], MR[:, :].unsqueeze(2).broadcast_to([128, 16, 32]), ALU.mult), t)
            yield
            on = SQ[:, :, :].rearrange("p h d -> p (h d)")
            A["sq"] = tt = turn(lambda c: on[:, 128 * c:128 * c + 128], 0, t)
            F[0] = t = act(lambda e: e.activation(oT[:, :, :], bank(0), ACT.Copy), tt, A.get("wo"))
            yield
            yield

            def wo(e):
                for c in range(4):
                    m = e.matmul(bank(1), oT[:, c, :], WA[:, 3, c, :], start=(c == 0), stop=(c == 3))
                return m
            A["wo"] = tp = pe(wo, F[1], t)
            F[1] = x1[b] = dve(lambda e: e.tensor_tensor(x, bank(1), x, ALU.add), tp)
            yield

        cx = sb(ax, "cx", [128, 2, 512])
        xm = sb(ax, "xm", [128, 512])
        sX = sb(ax, "sX", [128, 2])
        T1 = sb(ax, "T1", [128, 2, 512])
        HI = sb(ax, "HI", [128, 2, 2, 512], f32r)
        LO = sb(ax, "LO", [128, 2, 2, 512], f32r)
        vh = sb(ax, "vh", [128, 2, 4, 8, 32])
        NM = sb(ax, "NM", [128, 4, 4])
        NT = sb(ax, "NT", [4, 512], f32r)
        ox = sb(ax, "ox", [128, 512])
        rc = sb(ax, "rc", [128, 16, 32])
        R16 = sb(ax, "R16", [128, 16])
        bo = sb(ax, "bo", [128, 1])
        on2 = sb(ax, "on2", [128, 2, 512])
        x3 = sb(ax, "x3", [128, 512])
        x3T = sb(ax, "x3T", [128, 4, 128])
        t_vh = pool(lambda e: e.memset(vh[:, :, :, :, :], 0.0))
        t_vh = pool(lambda e: e.memset(vh[:, :, :, :, 16:17], 1.0), t_vh)
        cl = {}
        K = {}

        def bias_out(e):
            for hh in range(2):
                m = e.matmul(bank(7, 0, 1), WO[:, hh, :], BX[:, 4 + hh:5 + hh], start=(hh == 0), stop=(hh == 1))
            return m
        F[7] = t_bo = dve(lambda e: e.tensor_tensor(bo[:, :], bank(7, 0, 1), BX[:, 6:7], ALU.add), pe(bias_out, t_w))

        def load_c(b):
            cl[b] = load(f"d_c{b % 2}", cx[:, b % 2, :], I["ctx"][b, :, :], K.get(("v", b - 2)), K.get(("k", b - 2)))

        fbn = [0]

        def fb():
            fbn[0] += 1
            return 3 + fbn[0] % 2

        def prep(b):
            x = XB[:, b % NXB, :]
            d = b % 2
            c_ = cx[:, d, :]
            t_xm = yield from norm(x, xm[:, :], 1, sX, x1[b], K.get("xm"))
            for kq in range(2):
                src = c_ if kq == 0 else xm[:, :]
                tps = []
                for pm in range(2):
                    bk = fb()
                    tp = pe(lambda e, kq=kq, pm=pm, bk=bk, src=src: e.matmul(
                        bank(bk), WX[:, 2 * kq + pm, :], src, start=True, stop=True),
                        F[bk], t_w, cl[b] if kq == 0 else t_xm)
                    w, tab = 2 * kq + pm, (C_COS, C_SIN)[pm]
                    F[bk] = tb = dve(lambda e, w=w, pm=pm, bk=bk, tab=tab: e.scalar_tensor_tensor(
                        out=T1[:, pm, :], in0=bank(bk), scalar=BX[:, w:w + 1], in1=CST[:, tab:tab + 512],
                        op0=ALU.add, op1=ALU.mult), tp, K.get("T"))
                    yield
                K[("k", b) if kq == 0 else "xm"] = tp
                t = dve(lambda e: e.tensor_tensor(T1[:, 0, :], T1[:, 0, :], T1[:, 1, :], ALU.add), tb)
                yield
                th_ = act(lambda e, kq=kq: e.activation(HI[:, d, kq, :], T1[:, 0, :], ACT.Copy), t,
                          K.get(("stk", b - 2)))
                t = pool(lambda e, kq=kq: e.tensor_tensor(LO[:, d, kq, :], T1[:, 0, :],
                                                          HI[:, d, kq, :].bitcast(f32), ALU.subtract), th_)
                K["T"] = t
                K[("hl", b, kq)] = t
                if kq == 0:
                    for s2 in range(2):
                        bk = fb()

                        def go(e, s2=s2, bk=bk):
                            for i in range(2):
                                sc = 2 * s2 + i
                                m = e.matmul(bank(bk, 256 * i, 256 * i + 256), c_[:, 128 * sc:128 * sc + 128],
                                             WV[:, :], start=True, stop=True)
                            return m
                        tp = pe(go, F[bk], cl[b])
                        K[("v", b)] = tp
                        F[bk] = K[("vh", b)] = act(lambda e, s2=s2, bk=bk: e.activation(
                            vh[:, d, 2 * s2:2 * s2 + 2, :, 0:16].rearrange("p s h d -> p (s h) d"),
                            bank(bk).rearrange("p (s h) -> p s h", h=32)[:, :, 0:16],
                            ACT.Copy), tp, t_vh, K.get(("pv", b - 2)))
                        yield

        def front(b, hh):
            d = b % 2
            ready = {}

            def spread(j, kq):
                h, bk = 4 * hh + j, fb()
                wh, wl = ((W_KHI, W_KLO), (W_QHI, W_QLO))[kq]

                def go(e):
                    e.matmul(bank(bk), REP[:, h, 32 * wh:32 * wh + 128], HI[:, d, kq, :], start=True, stop=False)
                    return e.matmul(bank(bk), REP[:, h, 32 * wl:32 * wl + 128], LO[:, d, kq, :],
                                    start=False, stop=True)
                K[("stk", b)] = tp = pe(go, F[bk], K[("hl", b, kq)], t_rep)
                if kq == 0:
                    F[bk] = ready[j, 0] = dve(lambda e: e.tensor_scalar(
                        KS[:, h, :], bank(bk), CST[:, C_AB + 2:C_AB + 3], None, ALU.add),
                        tp, K.get(("st", hh)), t_rep)
                else:
                    F[bk] = ready[j, 1] = act(lambda e: e.activation(QS[:, h, :], bank(bk), ACT.Copy),
                                              tp, K.get(("st", hh)), t_rep)

            def top_of(j, qc):
                h, bk = 4 * hh + j, fb()
                tp = pe(lambda e: e.matmul(bank(bk), QS[:, h, 128 * qc:128 * qc + 128], KS[:, h, :],
                                           start=True, stop=True), F[bk], ready[j, 0], ready[j, 1])
                F[bk] = ready["m"] = dve(lambda e: e.tensor_reduce(
                    NM[:, qc, j:j + 1], bank(bk), AX.X, ALU.max, negate=True), tp, K.get("nmt"))

            spread(0, 0)
            spread(0, 1)
            yield
            for j in range(4):
                for qc in range(4):
                    top_of(j, qc)
                    if j < 3 and qc >= 2:
                        spread(j + 1, qc - 2)
                    yield
            bk = fb()

            def go(e):
                for qc in range(4):
                    m = e.transpose(ps[0:4, bk * 512 + 128 * qc:bk * 512 + 128 * qc + 128], NM[:, qc, :], ident)
                return m
            K["nmt"] = tt = pe(go, F[bk], ready["m"])
            F[bk] = t = dve(lambda e: e.tensor_copy(NT[:, :], ps[0:4, bk * 512:(bk + 1) * 512]), tt, K.get("ntd"))
            K["ntd"] = K[("qs", b, hh)] = P.put(
                "sp", lambda e: e.dma_start(QS[16:17, 4 * hh:4 * hh + 4, :].bitcast(f32), NT[:, :].bitcast(f32)),
                t, tt, sem="d_nt", by=16)
            yield

        pxf = [t_rep] * 4
        pxn = [0]

        later = []

        def apply():
            b, hh, sc, j, sl, te = later.pop(0)
            K["pv"] = K[("pv", b)] = pe(lambda e: e.matmul(
                ps[32 * j:32 * j + 32, 7 * 512:8 * 512], vh[:, b % 2, sc, 4 * hh + j, :], PX[:, sl, :],
                start=(sc == 0), stop=(sc == 3), tile_position=(0, 32 * j)), te, F[7] if sc == 0 else None,
                K[("vh", b)])
            pxf[sl] = K["pv"]

        def attend(b, hh):
            for sc in range(4):
                for j in range(4):
                    h = 4 * hh + j
                    bk = 5 + j % 2
                    sl = pxn[0] % 4
                    pxn[0] += 1
                    tp = pe(lambda e, h=h, sc=sc, bk=bk: e.matmul(
                        bank(bk), KS[:, h, 128 * sc:128 * sc + 128], QS[:, h, :], start=True, stop=True),
                        F[bk], K[("qs", b, hh)])
                    F[bk] = te = act(lambda e, bk=bk, sl=sl: e.activation(
                        PX[:, sl, :], bank(bk), ACT.Exp, scale=0.25), tp, pxf[sl])
                    later.append((b, hh, sc, j, sl, te))
                    K[("st", hh)] = tp
                    if sc * 4 + j >= 3:
                        apply()
                    yield

        def tail(b, hh):
            for _ in range(3):
                apply()
                if later and later[0][0:2] == (b, hh):
                    yield
            F[7] = t_o = act(lambda e: e.activation(ox[:, :], bank(7), ACT.Copy), K["pv"], K.get("ox"))
            yield
            yield
            bk = fb()

            def sums(e):
                for c in range(4):
                    m = e.matmul(bank(bk, 4 * c, 4 * c + 4), ox[:, 128 * c:128 * c + 128],
                                 CST[:, C_SEL:C_SEL + 128:32], start=True, stop=True)
                return m
            tb = pe(sums, F[bk], t_o)
            F[bk] = t = dve(lambda e: e.reciprocal(R16[:, :], bank(bk, 0, 16)), tb, K.get("r16"))
            K["r16"] = t = dve(lambda e: e.tensor_copy(
                rc[:, :, :], R16[:, :].unsqueeze(2).broadcast_to([128, 16, 32])), t, K.get("rc"))
            yield
            yield
            b2 = fb()
            K["rc"] = tb = turn(lambda c: rc[:, 4 * c:4 * c + 4, :], b2, t)
            F[b2] = K["ox"] = K[("on", hh)] = dve(lambda e: e.tensor_tensor(on2[:, hh, :], bank(b2), ox[:, :],
                                                                            ALU.mult), tb, K.get("wo"))
            yield

        def post_a(b):
            x = XB[:, b % NXB, :]
            yield
            yield
            bk = fb()

            def wo(e):
                for hh in range(2):
                    m = e.matmul(bank(bk), WO[:, hh, :], on2[:, hh, :], start=(hh == 0), stop=(hh == 1))
                return m
            K["wo"] = tp = pe(wo, F[bk], K[("on", 0)], K[("on", 1)])
            F[bk] = x2[b] = dve(lambda e: e.scalar_tensor_tensor(
                out=x, in0=bank(bk), scalar=bo[:, 0:1], in1=x, op0=ALU.add, op1=ALU.add), tp, t_bo)
            xs[b] = P.put("sp", lambda e: e.dma_start(XD[b, :, :], x), x2[b], sem=f"d_xs{b % 2}", by=16)
            yield

        def post_b(b):
            x = XB[:, b % NXB, :]
            x2[b] = t = yield from norm(x, x3[:, :], 1, ST3[:, b, :], x2[b], K.get("x3"))
            yield
            bk = fb()
            K["x3"] = tt = turn(lambda c: x3[:, c:512:4], bk, t)
            F[bk] = t = act(lambda e: e.activation(x3T[:, :, :], bank(bk), ACT.Copy), tt, K.get("x3T"))
            yield
            yield
            bg = fb()

            def gate(e):
                for c in range(4):
                    m = e.matmul(bank(bg, 0, 32), x3T[:, c, :], GW[:, c, :], start=(c == 0), stop=(c == 3))
                return m
            K["x3T"] = tp = pe(gate, F[bg], t)
            F[bg] = dve(lambda e: e.tensor_copy(LG[:, b, :], bank(bg, 0, 32)), tp)
            yield

        def drain(g):
            for _ in g:
                pass

        def weave(rounds, *gens):
            count = [0] * len(gens)
            for k in range(1, rounds + 1):
                for i, (g, n) in enumerate(gens):
                    while count[i] * rounds < k * (n or rounds):
                        count[i] += 1
                        next(g, None)
            for g, n in gens:
                if n is None:
                    drain(g)

        def chain(*gens):
            for g in gens:
                yield from g

        none = iter(())
        for b in range(4):
            load_x(b)
        load_c(0)
        load_c(1)
        drain(chainA(0))
        drain(prep(0))
        weave(36, (chainA(1), None), (front(0, 0), 18))
        for b in range(NB):
            ga = chainA(b + 2) if b + 2 < NB else iter(())
            more = b + 1 < NB
            weave(16, (chain(tail(b - 1, 1), post_a(b - 1), prep(b + 1) if more else none) if b
                       else prep(1), None),
                  (attend(b, 0), None), (front(b, 1), 22), (ga, AS))
            if b + 4 < NB:
                load_x(b + 4)
            if b + 2 < NB:
                load_c(b + 2)
            for z in range(8 * b, min(8 * b + 8, NSLOT // 128)):
                load("d_z", zrows[z, :, :], zt[:, :], t_z)
            weave(16, (chain(tail(b, 0), post_b(b - 1) if b else none), None),
                  (attend(b, 1), None), (front(b + 1, 0) if more else none, 22), (ga, AS))
            drain(ga)
        drain(chain(tail(NB - 1, 1), post_a(NB - 1), post_b(NB - 1)))

        P.fence(*P.last("pe", "act", "dve", "pool", "d_z", "d_cst", "d_xs0", "d_xs1"))
        ax.close()

        mo = ExitStack()
        rt = ExitStack()
        SI = sb(top, "SI", [128, NB, 8], i32)
        W6 = sb(top, "W6", [128, NB, 8])
        EB = sb(top, "EB", [1, NBLK], i32)
        G = sb(rt, "G", [128, NB, 10])
        G2 = sb(rt, "G2", [128, NB, 10])
        m8 = sb(rt, "m8", [128, NB, 8])
        KP = sb(rt, "KP", [128, NB, 4])
        LM = sb(rt, "LM", [128, NB, 34])
        LM2 = sb(rt, "LM2", [128, NB, 34])
        M = sb(rt, "M", [128, NB, 32])
        RM = sb(rt, "RM", [128, NB + 1, 32])
        SG = sb(rt, "SG", [128, NB, 32])
        SM = sb(rt, "SM", [128, NB])
        SV = sb(rt, "SV", [128, NB, 32])
        S8 = sb(rt, "S8", [128, NB, 8])
        junk = sb(rt, "junk", [128, 2, 32])
        ci = sb(rt, "ci", [128, 32], i32)
        nbf = sb(rt, "nbf", [128, 32])
        cu = sb(rt, "cu", [128, 2, 32])
        bs = sb(rt, "bs", [128, 32])
        GC = sb(rt, "GC", [128, 8, 512])
        E3 = GC[0:1, :, :].rearrange("p a n -> p (a n)")[:, 0:NBLK * 32].rearrange("p (b k) -> p b k", k=32)
        E1 = sb(rt, "E1", [1, NBLK])

        def step(fn, t, *a):
            return dve(fn, t, *a)

        Q = {}

        def routing():
            te = act(lambda e: e.activation(SG[:, :, :], LG[:, :, :], ACT.Exp, scale=-1.0))
            t = dve(lambda e: e.memset(G[:, :, :], BIG))
            dve(lambda e: e.memset(LM[:, :, :], BIG))
            t = step(lambda e: e.memset(RM[:, :, :], 0.0), t)
            t = step(lambda e: e.tensor_reduce(G[:, :, 0:4], LG[:, :, :].rearrange("p t (g k) -> p t g k", k=8),
                                               AX.X, ALU.max), t)
            for n in range(NB):
                t = step(lambda e, n=n: e.max(m8[:, n, :], G[:, n, :]), t)
                if n % 8 == 7:
                    yield
            for n in range(NB):
                t = step(lambda e, n=n: e.match_replace(G2[:, n, :], m8[:, n, :], G[:, n, :], -BIG), t)
                if n % 8 == 7:
                    yield
            t = step(lambda e: e.tensor_scalar(KP[:, :, :], G2[:, :, 0:4], -BIG, None, ALU.is_equal), t)
            t = step(lambda e: e.tensor_scalar(KP[:, :, :], KP[:, :, :], -1.0, 1e30, ALU.add, ALU.mult), t)
            t = step(lambda e: e.tensor_tensor(
                LM[:, :, 0:32].rearrange("p t (g k) -> p t g k", k=8), LG[:, :, :].rearrange("p t (g k) -> p t g k", k=8),
                KP[:, :, :].unsqueeze(3).broadcast_to([128, NB, 4, 8]), ALU.add), t)
            for n in range(NB):
                t = step(lambda e, n=n: e.max(m8[:, n, :], LM[:, n, :]), t)
                if n % 8 == 7:
                    yield
            for n in range(NB):
                t = step(lambda e, n=n: e.match_replace(LM2[:, n, :], m8[:, n, :], LM[:, n, :], -BIG), t)
                if n % 8 == 7:
                    yield
            t = step(lambda e: e.tensor_scalar(M[:, :, :], LM2[:, :, 0:32], -BIG, None, ALU.is_equal), t)
            for n in range(NB):
                t = step(lambda e, n=n: e.tensor_tensor(RM[:, n + 1, :], RM[:, n, :], M[:, n, :], ALU.add), t)

            yield

            for h in range(2):
                def rank(e, h=h):
                    e.matmul(bank(h), CST[:, C_TRI:C_TRI + 128], M[:, 16 * h:16 * h + 16, :], start=True, stop=False)
                    return e.matmul(bank(h), CST[:, C_ONE:C_ONE + 128], RM[:, 16 * h:16 * h + 16, :],
                                    start=False, stop=True)
                tr = pe(rank, t, F[h])
                F[h] = dve(lambda e, h=h: e.tensor_copy(SV[:, 16 * h:16 * h + 16, :], bank(h)), tr)
            tr = pe(lambda e: e.matmul(bank(0, 0, 32), CST[:, C_ONE:C_ONE + 128], RM[:, NB, :],
                                       start=True, stop=True), F[0])
            F[0] = t = step(lambda e: e.tensor_scalar(ci[:, :], bank(0, 0, 32), float(BLK - 1), None, ALU.add), tr)
            yield
            t = step(lambda e: e.tensor_scalar(SG[:, :, :], SG[:, :, :], 1.0, None, ALU.add), t, te)
            t = step(lambda e: e.reciprocal(SG[:, :, :], SG[:, :, :]), t)
            t = step(lambda e: e.tensor_tensor(SG[:, :, :], SG[:, :, :], M[:, :, :], ALU.mult), t)
            t = step(lambda e: e.tensor_reduce(SM[:, :], SG[:, :, :], AX.X, ALU.add), t)
            t = step(lambda e: e.reciprocal(SM[:, :], SM[:, :]), t)
            t = step(lambda e: e.tensor_tensor(SG[:, :, :], SG[:, :, :], SM[:, :].unsqueeze(2).broadcast_to([128, NB, 32]),
                                               ALU.mult), t)
            t = step(lambda e: e.tensor_scalar(ci[:, :], ci[:, :], 8, None, ALU.logical_shift_right), t)
            t = step(lambda e: e.tensor_copy(nbf[:, :], ci[:, :]), t)
            t = step(lambda e: e.tensor_copy(cu[:, 0, :], nbf[:, :]), t)
            for k in range(5):
                s, a, b_ = 1 << k, k % 2, 1 - k % 2
                dve(lambda e, s=s, a=a, b_=b_: e.tensor_copy(cu[:, b_, 0:s], cu[:, a, 0:s]), t)
                t = step(lambda e, s=s, a=a, b_=b_: e.tensor_tensor(cu[:, b_, s:32], cu[:, a, s:32], cu[:, a, 0:32 - s],
                                                                    ALU.add), t)
            t = step(lambda e: e.tensor_tensor(bs[:, :], cu[:, 1, :], nbf[:, :], ALU.subtract), t)
            t = step(lambda e: e.tensor_scalar(bs[:, :], bs[:, :], float(BLK), 1.0, ALU.mult, ALU.add), t)
            t = step(lambda e: e.tensor_tensor(SV[:, :, :], SV[:, :, :],
                                               bs[:, :].unsqueeze(1).broadcast_to([128, NB, 32]), ALU.add), t)
            t = step(lambda e: e.tensor_tensor(SV[:, :, :], SV[:, :, :], M[:, :, :], ALU.mult), t)
            for n in range(NB):
                t = step(lambda e, n=n: e.max(S8[:, n, :], SV[:, n, :]), t)
                if n % 8 == 7:
                    yield
            Q['si'] = t = step(lambda e: e.tensor_scalar(SI[:, :, :], S8[:, :, :], -1.0, None, ALU.add), t)
            t = step(lambda e: e.tensor_tensor(
                E3[:, :, :], cu[0:1, 1, :].unsqueeze(1).broadcast_to([1, NBLK, 32]),
                CST[0:1, C_BI:C_BI + NBLK].unsqueeze(2).broadcast_to([1, NBLK, 32]), ALU.is_le), t)
            t = step(lambda e: e.tensor_reduce(E1[:, :], E3[:, :, :], AX.X, ALU.add), t)
            Q['eb'] = t = step(lambda e: e.tensor_scalar(EB[:, :], E1[:, :], 31.0, None, ALU.min), t)
            jt = [None, None]
            for n in range(NB):
                for k in range(6):
                    q = k % 2
                    jt[q] = dve(lambda e, n=n, k=k, q=q: e.scalar_tensor_tensor(
                        out=junk[:, q, :], in0=SV[:, n, :], scalar=S8[:, n, k:k + 1], in1=SG[:, n, :],
                        op0=ALU.is_equal, op1=ALU.mult, accum_out=W6[:, n, k:k + 1]), t, jt[q])
                yield
            Q['w6'] = jt[:]

        WL = sb(mo, "WL", [128, 2, 2, 4, 352])
        DL = sb(mo, "DL", [128, 2, 3, 512])
        WG = [sb(mo, f"WG{i}", [128, 2, 2, 4, 352], f32r) for i in range(2)]
        WD = [sb(mo, f"WD{i}", [128, 2, 3, 512], f32r) for i in range(2)]
        NX = 4
        XI = sb(mo, "XI", [128, NX, 512])
        XC = sb(mo, "XC", [128, 2, 512])
        XT = sb(mo, "XT", [128, 2, 2, 512], f32r)
        HS = sb(mo, "HS", [128, 2, 352])
        HT = sb(mo, "HT", [128, 2, 2, 384], f32r)
        YO = sb(mo, "YO", [128, 4, 512])
        xif, xtf, yof = [None] * NX, [None] * 2, [None] * 4
        hsf, htf = [None, None], [None, None]
        sets = ["s0", "s1"] + list(range(NBLK)) + ["s0", "s1"]
        items = [("s", n, s, s) for n in range(PRE) for s in range(2)] + \
                [("m", b, i, b + 2) for b in range(NBLK) for i in range(2)] + \
                [("s", n, s, NBLK + 2 + s) for n in range(PRE, NB) for s in range(2)]
        N = len(items)
        last_use = {}
        for n, it in enumerate(items):
            last_use[it[3]] = n
        tin, txT, th, tht, src, xq = {}, {}, {}, {}, {}, {}
        tland, twt, tdone, tused = {}, {}, {}, {}
        landf = [[], []]
        regs = {}
        cnt = {"x": 0, "t": 0, "y": 0}
        slotted = []

        def land(k):
            q = k % 2
            if k >= len(sets):
                return
            w = sets[k]
            parts = []
            if isinstance(w, str):
                s = int(w[1])
                for i, name in enumerate(("sw_gate", "sw_up")):
                    parts.append(lambda e, i=i, name=name: e.dma_start(
                        WL[:, q, i, :, :], I[name][:, 352 * s:352 * s + 352].rearrange("(p c) n -> p c n", c=4)))
                parts.append(lambda e: e.dma_start(
                    DL[:, q, 0:2, :], I["sw_down"][352 * s:352 * s + 256, :].rearrange("(c p) n -> p c n", p=128)))
                parts.append(lambda e: e.dma_start(DL[0:96, q, 2, :], I["sw_down"][352 * s + 256:352 * s + 352, :]))
            else:
                def gate(e):
                    regs[w] = e.value_load(EB[0:1, w:w + 1], min_val=0, max_val=31)
                    return e.dma_start(WL[:, q, 0, :, :], I["w_gate"][bass.ds(regs[w], 1), :, :]
                                       .rearrange("a (p c) n -> p (a c) n", c=4))
                parts.append(gate)
                parts.append(lambda e: e.dma_start(WL[:, q, 1, :, :], I["w_up"][bass.ds(regs[w], 1), :, :]
                                                   .rearrange("a (p c) n -> p (a c) n", c=4)))
                parts.append(lambda e: e.dma_start(DL[:, q, 0:2, :], I["w_down"][bass.ds(regs[w], 1), 0:256, :]
                                                   .rearrange("a (c p) n -> p (a c) n", p=128)))
                parts.append(lambda e: e.dma_start(DL[0:96, q, 2, :], I["w_down"][bass.ds(regs[w], 1), 256:352, :]
                                                   .rearrange("a p n -> p (a n)")))
            for go in parts:
                tland[k] = P.put("sp", go, Q.get("eb") if not isinstance(w, str) else None, *landf[q],
                                 sem=f"d_wt{q}", by=16)

        def split(k):
            if k >= len(sets):
                return
            q = k % 2
            t0 = tland[k]
            free = tused[k - 2] if k >= 2 else None
            for w in range(2):
                for c in range(0, 4, 2):
                    ta = act(lambda e, w=w, c=c: e.activation(WG[q][:, 0, w, c:c + 2, :], WL[:, q, w, c:c + 2, :],
                                                              ACT.Copy), t0, free)
                    yield
                    tb = dve(lambda e, w=w, c=c: e.tensor_tensor(
                        WG[q][:, 1, w, c:c + 2, :], WL[:, q, w, c:c + 2, :],
                        WG[q][:, 0, w, c:c + 2, :].bitcast(f32), ALU.subtract), ta)
                    yield
            free = tdone[k - 2] if k >= 2 else None
            for r, c0, c1 in ((128, 0, 2), (96, 2, 3)):
                ta = act(lambda e, r=r, c0=c0, c1=c1: e.activation(WD[q][0:r, 0, c0:c1, :], DL[0:r, q, c0:c1, :],
                                                                   ACT.Copy), free)
                yield
                tb = dve(lambda e, r=r, c0=c0, c1=c1: e.tensor_tensor(
                    WD[q][0:r, 1, c0:c1, :], DL[0:r, q, c0:c1, :], WD[q][0:r, 0, c0:c1, :].bitcast(f32),
                    ALU.subtract), ta)
                yield
            twt[k] = (ta, tb)
            landf[q] = [ta, tb]

        def fetch(n):
            kind, a, i, k = items[n]
            if kind == "s" and i == 1:
                return
            sl = cnt["x"] % NX
            cnt["x"] += 1
            src[n] = sl
            if kind == "s":
                t = load(f"d_xi{sl}", XI[:, sl, :], XD[a, :, :], xif[sl])
                tin[n] = t
            else:
                tin[n] = load(f"d_xi{sl}", XI[:, sl, :], XS[BLK * a + 128 * i:BLK * a + 128 * i + 128, :],
                              xif[sl], *slotted)

        def s1(n):
            kind, a, i, k = items[n]
            if kind == "s" and i == 1:
                txT[n], src[n], xq[n] = txT[n - 1], src[n - 1], xq[n - 1]
                return
            q = xq[n] = cnt["t"] % 2
            cnt["t"] += 1
            sl = src[n]
            rows, t = XI[:, sl, :], tin[n]
            if kind == "s":
                rows = XC[:, q, :]
                t = dve(lambda e: e.tensor_scalar(rows, XI[:, sl, :], ST3[:, a, 0:1], ST3[:, a, 1:2],
                                                  ALU.subtract, ALU.mult), t, xcf[q])

            def go(e):
                for c in range(4):
                    m = e.transpose(bank(q, 128 * c, 128 * c + 128), rows[:, c:512:4], ident)
                return m
            tt = pe(go, F[q], t)
            if kind == "s":
                xcf[q] = tt
            else:
                xif[sl] = tt
            ta = act(lambda e: e.activation(XT[:, q, 0, :], bank(q), ACT.Copy), tt, xtf[q])
            F[q] = tb = dve(lambda e: e.tensor_tensor(XT[:, q, 1, :], bank(q), XT[:, q, 0, :].bitcast(f32),
                                                      ALU.subtract), ta)
            txT[n] = tb

        xcf = [None, None]

        def three(e, out_, lh, rh, first, last):
            e.matmul(out_, lh(0), rh(0), start=first, stop=False)
            e.matmul(out_, lh(0), rh(1), start=False, stop=False)
            return e.matmul(out_, lh(1), rh(0), start=False, stop=last)

        def s2(n):
            kind, a, i, k = items[n]
            q = n % 2
            bg, bu = 2 + q, 4 + q

            def go(e):
                for w in range(2):
                    for c in range(4):
                        m = three(e, bank(bg if w == 0 else bu, 0, 352),
                                  lambda p: XT[:, xq[n], p, 128 * c:128 * c + 128],
                                  lambda p: WG[k % 2][:, p, w, c, :], c == 0, c == 3)
                return m
            tp = pe(go, F[bg], F[bu], txT[n], *twt[k])
            xtf[xq[n]] = tp
            if last_use[k] == n:
                tused[k] = tp
            tg = act(lambda e: e.activation(HS[:, q, :], bank(bg, 0, 352), ACT.Silu), tp, hsf[q])
            F[bg] = tg
            th[n] = dve(lambda e: e.tensor_tensor(HS[:, q, :], bank(bu, 0, 352), HS[:, q, :], ALU.mult), tg)
            F[bu] = th[n]

        def s3(n):
            q = n % 2

            def go(e):
                for c in range(3):
                    r = 128 if c < 2 else 96
                    m = e.transpose(ps[0:r, 6 * 512 + 128 * c:6 * 512 + 128 * c + 128],
                                    HS[:, q, 128 * c:128 * c + r], ident)
                return m
            tt = pe(go, F[6], th[n])
            hsf[q] = tt
            for r, a, b in ((128, 0, 256), (96, 256, 384)):
                ta = act(lambda e, r=r, a=a, b=b: e.activation(
                    HT[0:r, q, 0, a:b], ps[0:r, 6 * 512 + a:6 * 512 + b], ACT.Copy), tt, htf[q])
            for r, a, b in ((128, 0, 256), (96, 256, 384)):
                tht[n] = dve(lambda e, r=r, a=a, b=b: e.tensor_tensor(
                    HT[0:r, q, 1, a:b], ps[0:r, 6 * 512 + a:6 * 512 + b], HT[0:r, q, 0, a:b].bitcast(f32),
                    ALU.subtract), ta)
            F[6] = tht[n]

        def s4(n):
            kind, a, i, k = items[n]
            q = n % 2

            def go(e):
                for c in range(3):
                    r = 128 if c < 2 else 96
                    m = three(e, bank(7), lambda p: HT[0:r, q, p, 128 * c:128 * c + 128],
                              lambda p: WD[k % 2][0:r, p, c, :],
                              c == 0 and not (kind == "s" and i == 1), c == 2 and not (kind == "s" and i == 0))
                return m
            tp = pe(go, F[7] if not (kind == "s" and i == 1) else None, tht[n])
            htf[q] = tp
            if last_use[k] == n:
                tdone[k] = tp
            if kind == "s" and i == 0:
                return
            yq = cnt["y"] % 4
            cnt["y"] += 1
            if kind == "s":
                sl = src[n]
                xif[sl] = F[7] = dve(lambda e: e.tensor_tensor(YO[:, yq, :], bank(7), XI[:, sl, :], ALU.add),
                                     tp, yof[yq])
                yof[yq] = P.put("act", lambda e: e.dma_start(YD[a, :, :], YO[:, yq, :]), F[7],
                                sem=f"d_y{yq}", by=16)
                yd[a] = yof[yq]
            else:
                F[7] = dve(lambda e: e.tensor_copy(YO[:, yq, :], bank(7)), tp, yof[yq])
                r0 = BLK * a + 128 * i
                yof[yq] = P.put("act", lambda e: e.dma_start(YS[r0:r0 + 128, :], YO[:, yq, :]), F[7],
                                sem=f"d_y{yq}", by=16)
                if n + 1 == N or items[n + 1][0] == "s":
                    stored.extend(yof)

        yd, stored = {}, []

        def scatter():
            fr = [[] for _ in range(4)]
            for n in range(NB):
                sl = n % 4
                t = P.put("pool", lambda e, n=n, sl=sl: e.dma_start(SC[:, sl, :], XD[n, :, :]),
                          Q["si"] if n == 0 else None, *fr[sl], sem=f"d_sx{sl}", by=16)
                t = pool(lambda e, n=n, sl=sl: e.tensor_scalar(
                    SC[:, sl, :], SC[:, sl, :], ST3[:, n, 0:1], ST3[:, n, 1:2], ALU.subtract, ALU.mult), t)
                for k in range(6):
                    ts = P.put("pool", lambda e, n=n, sl=sl, k=k: e.indirect_dma_start(
                        out=XS[:, :], out_offset=bass.IndirectOffsetOnAxis(ap=SI[:, n, k:k + 1], axis=0),
                        in_=SC[:, sl, :], in_offset=None), t, Q["si"], sem=f"d_sc{sl}", by=16)
                fr[sl] = [ts]
            slotted.extend(P.last(*[f"d_sc{q}" for q in range(4)]))

        SC = sb(mo, "SC", [128, 4, 512])

        def combine():
            g = 0
            for n in range(NB):
                xs_ = n % 2
                while n not in yd:
                    yield
                tx = load(f"d_cx{xs_}", CB[:, xs_, :], YD[n, :, :], yd[n], cbf[xs_])
                for k in range(6):
                    sl = g % NG
                    g += 1
                    tg = P.put("pool", lambda e, n=n, k=k, sl=sl: e.indirect_dma_start(
                        out=GB[:, sl, :], out_offset=None, in_=YS[:, :],
                        in_offset=bass.IndirectOffsetOnAxis(ap=SI[:, n, k:k + 1], axis=0)),
                        gf[sl], *stored, sem=f"d_g{sl}", by=16)
                    tx = gf[sl] = dve(lambda e, n=n, k=k, sl=sl, xs_=xs_: e.scalar_tensor_tensor(
                        out=CB[:, xs_, :], in0=GB[:, sl, :], scalar=W6[:, n, k:k + 1], in1=CB[:, xs_, :],
                        op0=ALU.mult, op1=ALU.add), tg, tx, *Q["w6"])
                    yield
                cbf[xs_] = P.put("sp", lambda e, n=n, xs_=xs_: e.dma_start(out[n, :, :], CB[:, xs_, :]), tx,
                                 sem=f"d_out{xs_}", by=16)

        NG = 6
        GB, CB = GC[:, 0:NG, :], GC[:, NG:NG + 2, :]
        gf, cbf = [None] * NG, [None] * 2

        land(0)
        land(1)
        for k in range(2):
            for _ in split(k):
                pass
        ro = routing()
        nf = 0

        def ahead(n):
            nonlocal nf
            while nf < min(n, N):
                fetch(nf)
                nf += 1
        ahead(2)
        s1(0)
        cb = None
        spl = iter(())
        mid = 2 * PRE
        for n in range(N + 1):
            if n < mid:
                for _ in range(-(-54 // (mid - 6))):
                    if next(ro, 1) == 1 and "w6" in Q and not slotted:
                        scatter()
                        land(2)
                        land(3)
            if n < N:
                ahead(n + 3 if n + 3 < mid or slotted else mid)
            if n < N and items[n][0] == "m" and items[n][2] == 0:
                k = items[n][3]
                for _ in spl:
                    pass
                spl = split(k + 1)
                if k + 2 not in tland:
                    land(k + 2)
            if n + 1 < N:
                s1(n + 1)
            if n >= 1:
                s3(n - 1)
            for _ in range(3):
                next(spl, None)
            if n < N:
                k = items[n][3]
                if k not in twt:
                    for _ in spl:
                        pass
                if k not in twt:
                    if k not in tland:
                        land(k)
                    for _ in split(k):
                        pass
                s2(n)
            for _ in range(3):
                next(spl, None)
            if n >= 1:
                s4(n - 1)
            if n == mid - 1:
                for _ in split(2):
                    pass
            if stored and cb is None:
                cb = combine()
            if cb is not None:
                for _ in range(4):
                    next(cb, None)
        for _ in cb:
            pass
        for xs_ in range(2):
            P.quiet("sp", lambda e, t=cbf[xs_]: e.wait_ge(sems[t[0]], t[1]))
        mo.close()
        rt.close()

        sems = {k: top.enter_context(nc.semaphore("s_" + k)) for k in P.count}
        block = top.enter_context(nc.Block())

        @block.tensor
        def _(e):
            P.emit("pe", e, sems)

        @block.scalar
        def _(e):
            P.emit("act", e, sems)

        @block.vector
        def _(e):
            P.emit("dve", e, sems)

        @block.gpsimd
        def _(e):
            P.emit("pool", e, sems)

        @block.sync
        def _(e):
            P.emit("sp", e, sems)


def constants():
    c = np.zeros((128, C_N), np.float32)
    p = np.arange(128)
    c[:, C_ID:C_ID + 128] = np.eye(128)
    c[:, C_TRI:C_TRI + 128] = p[:, None] < p[None, :]
    c[:, C_ONE:C_ONE + 128] = 1.0
    c[:, C_SEL:C_SEL + 128] = p[:, None] == (p[None, :] // 32) * 32 + 16
    inv = (np.float32(1.0) / np.float32(10000.0) ** (np.arange(0, 16, 2, dtype=np.float32) / np.float32(16))
           ).astype(np.float32)
    pos = (np.arange(512, dtype=np.float32)[:, None] * inv[None, :]).astype(np.float32)
    cos, sin = np.cos(pos).astype(np.float32), np.sin(pos).astype(np.float32)
    for r in range(128):
        d = r % 16
        c[r, C_COS:C_COS + 512] = cos[:, d % 8]
        c[r, C_SIN:C_SIN + 512] = -sin[:, d % 8] if d < 8 else sin[:, d % 8]
    c[:, C_MSK:C_MSK + 128] = np.where(p[None, :] > p[:, None], -1e30, 0.0)
    c[:, C_AB] = p % 32 < 16
    c[:, C_AB + 1] = p % 32 >= 16
    c[16, C_AB + 2] = 1.0
    c[:, C_BI:C_BI + 128] = p[None, :]
    return c


def spreading():
    r = np.zeros((128, 8, 320), np.float32)
    for h in range(8):
        for n, on in enumerate(SPREAD):
            for d in range(16 if on else 0):
                r[16 * h + d, h, 32 * n + d] = 1.0
    return r


def laid_out(inputs):
    g = {k: np.asarray(v) for k, v in inputs.items()}
    swap = np.concatenate([np.arange(8, 16), np.arange(0, 8)])
    Wk, Wq = g["L0_xattn_Wk"], g["L0_xattn_Wq"]
    wx = np.zeros((128, 4, 128), np.float32)
    bx = np.zeros((128, 7), np.float32)
    wv = np.zeros((128, 256), np.float32)
    wo = np.zeros((128, 2, 128), np.float32)
    turned = (np.arange(8)[:, None] * 16 + swap[None, :]).ravel()
    for kq, (W, b) in enumerate(((Wk, g["L0_xattn_bk"]), (Wq, g["L0_xattn_bq"]))):
        for pm, r in enumerate((np.arange(128), turned)):
            wx[:, 2 * kq + pm, :] = W[r, :].T
            bx[:, 2 * kq + pm] = b[r]
    for hh in range(2):
        for j in range(4):
            rows = 16 * (4 * hh + j) + np.arange(16)
            wv[:, 128 * hh + 32 * j:128 * hh + 32 * j + 16] = g["L0_xattn_Wv"][rows, :].T
            wo[32 * j:32 * j + 16, hh, :] = g["L0_xattn_Wo"][:, rows].T
            bx[32 * j:32 * j + 16, 4 + hh] = g["L0_xattn_bv"][rows]
    bx[:, 6] = g["L0_xattn_bo"]
    a = {
        "x": g["x"], "ctx": g["ctx_2048"], "cst": constants(), "rep": spreading(), "wx": wx, "wv": wv, "wo": wo, "bx": bx,
        "Wq": g["L0_attn_Wq"], "Wk": g["L0_attn_Wk"], "Wv": g["L0_attn_Wv"], "Wo": g["L0_attn_Wo"],
        "lq": np.stack([g["L0_attn_lq1"], g["L0_attn_lk1"], g["L0_attn_lq2"], g["L0_attn_lk2"]]),
        "gate_w": g["L0_ffn_gate_w"], "w_gate": g["L0_ffn_w_gate"], "w_up": g["L0_ffn_w_up"],
        "w_down": g["L0_ffn_w_down"], "sw_gate": g["L0_ffn_sw_gate"], "sw_up": g["L0_ffn_sw_up"],
        "sw_down": g["L0_ffn_sw_down"],
    }
    return {k: np.ascontiguousarray(v) for k, v in a.items()}


def kernel(**inputs):
    import concourse.bacc as bacc
    from concourse.bass_utils import run_bass_kernel_spmd

    nc = bacc.Bacc("TRN2", target_bir_lowering=False, num_devices=1)
    arrays, aps = {}, {}
    for name, a in laid_out(inputs).items():
        arrays[f"in_{name}"] = a
        aps[name] = nc.dram_tensor(f"in_{name}", a.shape, mybir.dt.from_np(a.dtype), kind="ExternalInput").ap()
    out = nc.dram_tensor("out_0", (NB, 128, 512), mybir.dt.float32, kind="ExternalOutput").ap()
    build(nc, aps, out)
    r = run_bass_kernel_spmd(nc, [arrays], core_ids=[0])
    return r.results[0]["out_0"]
```

```python
import math
import numpy as np
import concourse.bass as bass
from concourse import mybir
from contextlib import ExitStack

NB = 32
BLK = 256
NBLK = 127
ROOM = 4096
NROW = 32 * ROOM
LAMBDA_INIT = 0.8 - 0.6 * math.exp(-0.3 * 12)
BIG = 3.0e38
C_ID, C_TRI, C_ONE, C_SEL, C_COS, C_SIN, C_MSK, C_AB, C_BI = 0, 128, 256, 384, 512, 1024, 1536, 1664, 1667
C_BA = C_BI + 1
C_N = C_BA + 32
SPREAD = (0, 0, 1, 1, 0, 0, 1, 0, 1, 0)
W_KHI, W_KLO, W_QHI, W_QLO = 6, 5, 2, 0
NXB = 6
AS = 17
PRE = 4


class Plan:

    def __init__(self):
        self.lists = {n: [] for n in ("pe", "act", "dve", "pool", "sp")}
        self.count = {}
        self.base = {n: [] for n in self.lists}

    def put(self, eng, fn, *after, sem=None, by=1):
        key = sem or eng
        self.count[key] = self.count.get(key, 0) + by
        self.lists[eng].append((self.base[eng] + list(after), fn, key, by))
        self.base[eng] = []
        return (key, self.count[key])

    def quiet(self, eng, fn, *after):
        self.lists[eng].append((self.base[eng] + list(after), fn, None, 0))
        self.base[eng] = []

    def fence(self, *tokens):
        for n in self.base:
            self.base[n] = list(tokens)

    def last(self, *keys):
        return [(k, self.count[k]) for k in keys if self.count.get(k)]

    def emit(self, name, eng, sems):
        seen = {}
        for after, fn, key, by in self.lists[name]:
            for t in after:
                if t is not None and seen.get(t[0], 0) < t[1]:
                    eng.wait_ge(sems[t[0]], t[1])
                    seen[t[0]] = t[1]
            ins = fn(eng)
            if key:
                ins.then_inc(sems[key], by)


def build(nc, I, out):
    f32, f32r, bf16, i32 = mybir.dt.float32, mybir.dt.float32r, mybir.dt.bfloat16, mybir.dt.int32
    ALU, ACT, AX = mybir.AluOpType, mybir.ActivationFunctionType, mybir.AxisListType
    P = Plan()

    def pe(fn, *a): return P.put("pe", fn, *a)
    def act(fn, *a): return P.put("act", fn, *a)
    def dve(fn, *a): return P.put("dve", fn, *a)
    def pool(fn, *a): return P.put("pool", fn, *a)
    def load(sem, dst, src, *a, eng="sp"):
        return P.put(eng, lambda e: e.dma_start(dst, src), *a, sem=sem, by=16)

    top = ExitStack()
    with top:
        def sb(stack, name, shape, dt=f32):
            return stack.enter_context(nc.sbuf_tensor(name, shape, dt))

        XS = nc.dram_tensor("xs_sorted", (NROW, 512), f32, kind="Internal").ap()
        YS = nc.dram_tensor("ys_sorted", (NBLK * BLK, 512), f32, kind="Internal").ap()

        ps = top.enter_context(nc.psum_tensor("ps", [128, 8 * 512], f32))

        def bank(i, a=0, b=512):
            return ps[:, i * 512 + a:i * 512 + b]

        XD = nc.dram_tensor("x_after", (NB, 128, 512), f32, kind="Internal").ap()
        YD = nc.dram_tensor("x_shared", (NB, 128, 512), f32, kind="Internal").ap()
        CST = sb(top, "CST", [128, C_N])
        ident = CST[:, C_ID:C_ID + 128]
        ST3 = sb(top, "ST3", [128, NB, 2])
        F = [None] * 8

        t_cst = load("d_cst", CST[:, :], I["cst"])
        mh = sb(top, "mh", [128, 16])
        zt = sb(top, "zt", [128, 1024])
        SI = sb(top, "SI", [128, NB, 8], i32)
        SV = sb(top, "SV", [128, NB, 32])
        W6 = sb(top, "W6", [128, NB, 8])
        RM = sb(top, "RM", [128, 2, 32])
        t_mh = pool(lambda e: e.memset(mh[:, :], -0.5))

        ax = ExitStack()
        XB = sb(ax, "XB", [128, NXB, 512])
        WA = sb(ax, "WA", [128, 4, 4, 512])
        WX = sb(ax, "WX", [128, 4, 128])
        WV = sb(ax, "WV", [128, 256])
        WO = sb(ax, "WO", [128, 2, 128])
        BX = sb(ax, "BX", [128, 7])
        GW = sb(ax, "GW", [128, 4, 32])
        LQ = sb(ax, "LQ", [128, 4, 16])
        idb = sb(ax, "idb", [128, 128], bf16)
        mkb = sb(ax, "mkb", [128, 4, 128], bf16)
        REP = sb(ax, "REP", [128, 8, 320], f32r)
        KS = sb(ax, "KS", [128, 8, 512], f32r)
        QS = sb(ax, "QS", [128, 8, 512], f32r)
        for n, w in enumerate(("Wq", "Wk", "Wv", "Wo")):
            load("d_w", WA[:, n, :, :], I[w].rearrange("(c p) n -> p c n", p=128))
        load("d_w", WX[:, :, :], I["wx"])
        load("d_w", WV[:, :], I["wv"])
        load("d_w", WO[:, :, :], I["wo"])
        load("d_w", BX[:, :], I["bx"])
        load("d_w", GW[:, :, :], I["gate_w"].rearrange("(p c) n -> p c n", c=4))
        t_w = load("d_w", LQ[:, :, :], I["lq"].partition_broadcast(128))

        t_idb = dve(lambda e: e.tensor_copy(idb[:, :], ident), t_cst)
        t_mkb = dve(lambda e: e.tensor_copy(
            mkb[:, :, :], CST[:, C_MSK:C_MSK + 128].unsqueeze(1).broadcast_to([128, 4, 128])), t_cst)
        PX = sb(ax, "PX", [128, 4, 512])
        RT = PX[:, 0:2, :]
        t_rep = []
        for h in range(8):
            q = h % 2
            t = load(f"d_rt{q}", RT[:, q, 0:320], I["rep"][:, h, :], t_rep[h - 2] if h >= 2 else None)
            t_rep.append(dve(lambda e, h=h, q=q: e.tensor_copy(REP[:, h, :], RT[:, q, 0:320]), t))
        t_rep = t_rep[-1]
        lm = sb(ax, "lm", [128, 2, 16])
        ls = sb(ax, "ls", [128, 2])
        le = sb(ax, "le", [128, 2])
        neglam = sb(ax, "neglam", [128, 1])
        t = dve(lambda e: e.tensor_tensor(lm[:, :, :], LQ[:, 0:4:2, :], LQ[:, 1:4:2, :], ALU.mult), t_w)
        t = dve(lambda e: e.tensor_reduce(ls[:, :], lm[:, :, :], AX.X, ALU.add), t)
        t = act(lambda e: e.activation(le[:, :], ls[:, :], ACT.Exp), t)
        t = dve(lambda e: e.tensor_tensor(neglam[:, :], le[:, 1:2], le[:, 0:1], ALU.subtract), t)
        t_lam = dve(lambda e: e.tensor_scalar(neglam[:, :], neglam[:, :], -LAMBDA_INIT, None, ALU.add), t)

        t_z = pool(lambda e: e.memset(zt[:, :], 0.0))
        zrows = [XS[ROOM * x_:ROOM * x_ + BLK, :].rearrange("(p i) d -> p (i d)", i=2) for x_ in range(32)]

        st6 = sb(ax, "st6", [128, 2, 6])
        mv = sb(ax, "mv", [128, 2, 2])
        ve = sb(ax, "ve", [128, 2, 1])
        lnfree = [None, None]

        def norm(x, dst, which, stats, *after):
            s, m, v = st6[:, which, :], mv[:, which, :], ve[:, which, :]
            t = dve(lambda e: e.bn_stats(s, x), *after, lnfree[which])
            t = dve(lambda e: e.bn_aggr(m, s), t)
            t = pool(lambda e: e.tensor_scalar(v, m[:, 1:2], 1e-5, None, ALU.add), t, t_mh)
            t = pool(lambda e: e.tensor_tensor(stats[:, 1:2], v, mh[:, 0:1], ALU.pow), t)
            t = pool(lambda e: e.tensor_copy(stats[:, 0:1], m[:, 0:1]), t)
            yield
            yield
            lnfree[which] = t = dve(lambda e: e.tensor_scalar(dst, x, stats[:, 0:1], stats[:, 1:2],
                                                              ALU.subtract, ALU.mult), t)
            return t

        def turn(src, b, *after):
            def go(e):
                for c in range(4):
                    m = e.transpose(bank(b, 128 * c, 128 * c + 128), src(c), ident)
                return m
            return pe(go, F[b], *after, t_cst)

        xn = sb(ax, "xn", [128, 512])
        sA = sb(ax, "sA", [128, 2])
        xT = sb(ax, "xT", [128, 4, 128])
        qA = sb(ax, "qA", [128, 4, 128])
        qB = sb(ax, "qB", [128, 4, 128])
        kT = sb(ax, "kT", [128, 4, 128])
        vA = sb(ax, "vA", [128, 512])
        nm = sb(ax, "nm", [128, 8])
        nb4 = sb(ax, "nb4", [128, 8])
        PA = sb(ax, "PA", [128, 8, 128])
        SU = sb(ax, "SU", [128, 32])
        RS = sb(ax, "RS", [128, 4, 4])
        CC = sb(ax, "CC", [128, 4, 4])
        aw = sb(ax, "aw", [128, 4, 128])
        awT = sb(ax, "awT", [128, 4, 128])
        R1 = sb(ax, "R1", [128, 4, 4])
        OA = sb(ax, "OA", [128, 16, 32])
        SQ = sb(ax, "SQ", [128, 16, 32])
        MS = sb(ax, "MS", [128, 16])
        MR = sb(ax, "MR", [128, 16])
        oT = sb(ax, "oT", [128, 4, 128])
        xl = {}
        x1 = {}
        x2, xs = {}, {}
        A = {}

        def load_x(b):
            xl[b] = load(f"d_x{b % NXB}", XB[:, b % NXB, :], I["x"][b, :, :], x2.get(b - NXB), xs.get(b - NXB))

        def chainA(b):
            x = XB[:, b % NXB, :]
            t_xn = yield from norm(x, xn[:, :], 0, sA, xl[b], A.get("xn"))
            yield
            A["xn"] = tt = turn(lambda c: xn[:, 128 * c:128 * c + 128], 0, t_xn)
            F[0] = t_xT = act(lambda e: e.activation(xT[:, :, :], bank(0), ACT.Copy), tt, A.get("xT"))
            yield
            yield

            def proj(b_, w):
                def go(e):
                    for ct in range(4):
                        for c in range(4):
                            m = e.matmul(bank(b_, 128 * ct, 128 * ct + 128),
                                         WA[:, w, c, 128 * ct:128 * ct + 128], xT[:, c, :],
                                         start=(c == 0), stop=(c == 3))
                    return m
                return pe(go, F[b_], t_xT, t_w)

            tq = proj(1, 0)
            yield
            t1 = act(lambda e: e.activation(qA[:, :, :], bank(1), ACT.Copy, scale=CST[:, C_AB:C_AB + 1]),
                     tq, A.get("s"))
            tk = proj(2, 1)
            yield
            F[1] = t2 = dve(lambda e: e.tensor_scalar(qB[:, :, :], bank(1), CST[:, C_AB + 1:C_AB + 2], None,
                                                      ALU.mult), tq, t1, A.get("s"))
            F[2] = t3 = act(lambda e: e.activation(kT[:, :, :], bank(2), ACT.Copy), tk, A.get("s"))

            def values(e):
                for c in range(4):
                    m = e.matmul(bank(0), xT[:, c, :], WA[:, 2, c, :], start=(c == 0), stop=(c == 3))
                return m
            A["xT"] = tv = pe(values, F[0], t_xT)
            yield
            F[0] = t4 = act(lambda e: e.activation(vA[:, :], bank(0), ACT.Copy), tv, A.get("pv"))
            S = ps[:, 512:1536].rearrange("p (h k) -> p h k", k=128)
            done = {}

            def scores(u):
                def sc(e):
                    for r in range(2):
                        e.matmul(bank(1 + r), idb[:, :], mkb[:, :, :], start=True, stop=False,
                                 skip_group_check=True)
                    for i in range(2):
                        for hf in range(2):
                            for r in range(2):
                                q, j, ct = (qB if hf else qA), 2 * (u % 2) + r, 2 * (u // 2) + i
                                col = i * 256 + hf * 128
                                m = e.matmul(bank(1 + r, col, col + 128), q[32 * j:32 * j + 32, ct, :],
                                             kT[32 * j:32 * j + 32, ct, :], start=False,
                                             stop=i == 1 and hf == 1, skip_group_check=True)
                    return m
                A["s"] = pe(sc, F[1], F[2], t1, t2, t3, t_idb, t_mkb)

            def tops(u):
                A["nm"] = tm = dve(lambda e: e.tensor_reduce(nm[:, :], S, AX.X, ALU.max, negate=True),
                                   A["s"], A.get("nm"))
                A["nm"] = done["m", u] = dve(lambda e: e.tensor_scalar(nb4[:, :], nm[:, :], 0.25, None, ALU.mult),
                                             tm, A.get("nb4"))

            def exps(u, part):
                for h in range(4 * part, 4 * part + 4):
                    te = act(lambda e, h=h: e.activation(
                        PA[:, h, :], S[:, h, :], ACT.Exp, bias=nb4[:, h:h + 1], scale=0.25,
                        accum_out=SU[:, 8 * u + h:8 * u + h + 1]), done["m", u], A.get("aw"), A.get("o1"))
                F[1] = F[2] = A["nb4"] = done["e", u] = te

            def weigh(u):
                te = done["e", u]
                s1, s2 = SU[:, 8 * u:8 * u + 8:2], SU[:, 8 * u + 1:8 * u + 8:2]
                tr = dve(lambda e: e.reciprocal(RS[:, u, :], s2), te)
                done["r", u] = dve(lambda e: e.reciprocal(R1[:, u, :], s1), te, A.get("oa"))
                tc = dve(lambda e: e.scalar_tensor_tensor(
                    out=CC[:, u, :], in0=s1, scalar=neglam[:, 0:1], in1=RS[:, u, :], op0=ALU.mult, op1=ALU.mult),
                    tr, t_lam)
                for j in range(4):
                    ta = dve(lambda e, j=j: e.scalar_tensor_tensor(
                        out=aw[:, j, :], in0=PA[:, 2 * j + 1, :], scalar=CC[:, u, j:j + 1], in1=PA[:, 2 * j, :],
                        op0=ALU.mult, op1=ALU.add), tc, A.get("awf"))
                A["aw"] = ta

            def turned(u):
                A["awf"] = tt = turn(lambda c: aw[:, c, :], 0, A["aw"])
                F[0] = done["t", u] = act(lambda e: e.activation(awT[:, :, :], bank(0), ACT.Copy), tt, A.get("pv"))

            def values_of(u):
                def pv(e):
                    for j in range(4):
                        h = 4 * (2 * (u // 2) + j % 2) + 2 * (u % 2) + j // 2
                        m = e.matmul(bank(0, 32 * j, 32 * j + 32), awT[:, j, :], vA[:, 32 * h:32 * h + 32],
                                     start=True, stop=True)
                    return m
                A["pv"] = pe(pv, F[0], done["t", u], t4)

            def scaled(u):
                F[0] = A["o1"] = done["o", u] = dve(lambda e: e.tensor_tensor(
                    OA[:, 8 * (u // 2):8 * (u // 2) + 8, :]
                    .rearrange("p (i s r) d -> p s r i d", i=2, s=2)[:, u % 2, :, :, :],
                    bank(0, 0, 128).rearrange("p (r i d) -> p r i d", r=2, i=2),
                    R1[:, u, :].rearrange("p (r i) -> p r i", r=2).unsqueeze(3).broadcast_to([128, 2, 2, 32]),
                    ALU.mult), A["pv"], done["r", u], A.get("oa"))

            scores(0)
            yield
            tops(0)
            yield
            exps(0, 0)
            yield
            exps(0, 1)
            yield
            for u in range(4):
                if u:
                    scaled(u - 1)
                weigh(u)
                if u < 3:
                    scores(u + 1)
                yield
                turned(u)
                if u < 3:
                    tops(u + 1)
                yield
                if u < 3:
                    exps(u + 1, 0)
                yield
                values_of(u)
                if u < 3:
                    exps(u + 1, 1)
                    yield
            scaled(3)
            to = done["o", 3]
            t = act(lambda e: e.activation(SQ[:, :, :], OA[:, :, :], ACT.Square), to, A.get("sq"))
            yield
            t = dve(lambda e: e.tensor_reduce(MS[:, :], SQ[:, :, :], AX.X, ALU.add), t)
            t = pool(lambda e: e.tensor_scalar(MS[:, :], MS[:, :], 1.0 / 32, 1e-5, ALU.mult, ALU.add), t)
            t = pool(lambda e: e.tensor_tensor(MR[:, :], MS[:, :], mh[:, :], ALU.pow), t)
            t = pool(lambda e: e.tensor_scalar(MR[:, :], MR[:, :], 1.0 - LAMBDA_INIT, None, ALU.mult), t)
            yield
            yield
            yield
            A["oa"] = t = dve(lambda e: e.tensor_tensor(
                SQ[:, :, :], OA[:, :, :], MR[:, :].unsqueeze(2).broadcast_to([128, 16, 32]), ALU.mult), t)
            yield
            on = SQ[:, :, :].rearrange("p h d -> p (h d)")
            A["sq"] = tt = turn(lambda c: on[:, 128 * c:128 * c + 128], 0, t)
            F[0] = t = act(lambda e: e.activation(oT[:, :, :], bank(0), ACT.Copy), tt, A.get("wo"))
            yield
            yield

            def wo(e):
                for c in range(4):
                    m = e.matmul(bank(1), oT[:, c, :], WA[:, 3, c, :], start=(c == 0), stop=(c == 3))
                return m
            A["wo"] = tp = pe(wo, F[1], t)
            F[1] = x1[b] = dve(lambda e: e.tensor_tensor(x, bank(1), x, ALU.add), tp)
            yield

        cx = sb(ax, "cx", [128, 2, 512])
        xm = sb(ax, "xm", [128, 512])
        sX = sb(ax, "sX", [128, 2])
        T1 = sb(ax, "T1", [128, 2, 512])
        HI = sb(ax, "HI", [128, 2, 2, 512], f32r)
        LO = sb(ax, "LO", [128, 2, 2, 512], f32r)
        vh = sb(ax, "vh", [128, 2, 4, 8, 32])
        NM = sb(ax, "NM", [128, 4, 4])
        NT = sb(ax, "NT", [4, 512], f32r)
        ox = sb(ax, "ox", [128, 512])
        rc = sb(ax, "rc", [128, 16, 32])
        R16 = sb(ax, "R16", [128, 16])
        bo = sb(ax, "bo", [128, 1])
        on2 = sb(ax, "on2", [128, 2, 512])
        x3 = sb(ax, "x3", [128, 2, 512])
        G = sb(ax, "G", [128, 10])
        G2 = sb(ax, "G2", [128, 10])
        m8 = sb(ax, "m8", [128, 8])
        KP = sb(ax, "KP", [128, 4])
        LM = sb(ax, "LM", [128, 34])
        LM2 = sb(ax, "LM2", [128, 34])
        M = sb(ax, "M", [128, 32])
        SG = sb(ax, "SG", [128, 32])
        SM = sb(ax, "SM", [128, 1])
        S8 = sb(ax, "S8", [128, 8])
        junk = sb(ax, "junk", [128, 2, 32])
        dve(lambda e: e.memset(G[:, :], BIG))
        dve(lambda e: e.memset(LM[:, :], BIG))
        t_pad = dve(lambda e: e.memset(RM[:, :, :], 0.0))
        x3T = sb(ax, "x3T", [128, 4, 128])
        t_vh = pool(lambda e: e.memset(vh[:, :, :, :, :], 0.0))
        t_vh = pool(lambda e: e.memset(vh[:, :, :, :, 16:17], 1.0), t_vh)
        cl = {}
        K = {}

        def bias_out(e):
            for hh in range(2):
                m = e.matmul(bank(7, 0, 1), WO[:, hh, :], BX[:, 4 + hh:5 + hh], start=(hh == 0), stop=(hh == 1))
            return m
        F[7] = t_bo = dve(lambda e: e.tensor_tensor(bo[:, :], bank(7, 0, 1), BX[:, 6:7], ALU.add), pe(bias_out, t_w))

        def load_c(b):
            cl[b] = load(f"d_c{b % 2}", cx[:, b % 2, :], I["ctx"][b, :, :], K.get(("v", b - 2)), K.get(("k", b - 2)))

        fbn = [0]

        def fb():
            fbn[0] += 1
            return 3 + fbn[0] % 2

        def prep(b):
            x = XB[:, b % NXB, :]
            d = b % 2
            c_ = cx[:, d, :]
            t_xm = yield from norm(x, xm[:, :], 1, sX, x1[b], K.get("xm"))
            for kq in range(2):
                src = c_ if kq == 0 else xm[:, :]
                tps = []
                for pm in range(2):
                    bk = fb()
                    tp = pe(lambda e, kq=kq, pm=pm, bk=bk, src=src: e.matmul(
                        bank(bk), WX[:, 2 * kq + pm, :], src, start=True, stop=True),
                        F[bk], t_w, cl[b] if kq == 0 else t_xm)
                    w, tab = 2 * kq + pm, (C_COS, C_SIN)[pm]
                    F[bk] = tb = dve(lambda e, w=w, pm=pm, bk=bk, tab=tab: e.scalar_tensor_tensor(
                        out=T1[:, pm, :], in0=bank(bk), scalar=BX[:, w:w + 1], in1=CST[:, tab:tab + 512],
                        op0=ALU.add, op1=ALU.mult), tp, K.get("T"))
                    yield
                K[("k", b) if kq == 0 else "xm"] = tp
                t = dve(lambda e: e.tensor_tensor(T1[:, 0, :], T1[:, 0, :], T1[:, 1, :], ALU.add), tb)
                yield
                th_ = act(lambda e, kq=kq: e.activation(HI[:, d, kq, :], T1[:, 0, :], ACT.Copy), t,
                          K.get(("stk", b - 2)))
                t = pool(lambda e, kq=kq: e.tensor_tensor(LO[:, d, kq, :], T1[:, 0, :],
                                                          HI[:, d, kq, :].bitcast(f32), ALU.subtract), th_)
                K["T"] = t
                K[("hl", b, kq)] = t
                if kq == 0:
                    for s2 in range(2):
                        bk = fb()

                        def go(e, s2=s2, bk=bk):
                            for i in range(2):
                                sc = 2 * s2 + i
                                m = e.matmul(bank(bk, 256 * i, 256 * i + 256), c_[:, 128 * sc:128 * sc + 128],
                                             WV[:, :], start=True, stop=True)
                            return m
                        tp = pe(go, F[bk], cl[b])
                        K[("v", b)] = tp
                        F[bk] = K[("vh", b)] = act(lambda e, s2=s2, bk=bk: e.activation(
                            vh[:, d, 2 * s2:2 * s2 + 2, :, 0:16].rearrange("p s h d -> p (s h) d"),
                            bank(bk).rearrange("p (s h) -> p s h", h=32)[:, :, 0:16],
                            ACT.Copy), tp, t_vh, K.get(("pv", b - 2)))
                        yield

        def front(b, hh):
            d = b % 2
            ready = {}

            def spread(j, kq):
                h, bk = 4 * hh + j, fb()
                wh, wl = ((W_KHI, W_KLO), (W_QHI, W_QLO))[kq]

                def go(e):
                    e.matmul(bank(bk), REP[:, h, 32 * wh:32 * wh + 128], HI[:, d, kq, :], start=True, stop=False)
                    return e.matmul(bank(bk), REP[:, h, 32 * wl:32 * wl + 128], LO[:, d, kq, :],
                                    start=False, stop=True)
                K[("stk", b)] = tp = pe(go, F[bk], K[("hl", b, kq)], t_rep)
                if kq == 0:
                    F[bk] = ready[j, 0] = dve(lambda e: e.tensor_scalar(
                        KS[:, h, :], bank(bk), CST[:, C_AB + 2:C_AB + 3], None, ALU.add),
                        tp, K.get(("st", hh)), t_rep)
                else:
                    F[bk] = ready[j, 1] = act(lambda e: e.activation(QS[:, h, :], bank(bk), ACT.Copy),
                                              tp, K.get(("st", hh)), t_rep)

            def top_of(j, qc):
                h, bk = 4 * hh + j, fb()
                tp = pe(lambda e: e.matmul(bank(bk), QS[:, h, 128 * qc:128 * qc + 128], KS[:, h, :],
                                           start=True, stop=True), F[bk], ready[j, 0], ready[j, 1])
                F[bk] = ready["m"] = dve(lambda e: e.tensor_reduce(
                    NM[:, qc, j:j + 1], bank(bk), AX.X, ALU.max, negate=True), tp, K.get("nmt"))

            spread(0, 0)
            spread(0, 1)
            yield
            for j in range(4):
                for qc in range(4):
                    top_of(j, qc)
                    if j < 3 and qc >= 2:
                        spread(j + 1, qc - 2)
                    yield
            bk = fb()

            def go(e):
                for qc in range(4):
                    m = e.transpose(ps[0:4, bk * 512 + 128 * qc:bk * 512 + 128 * qc + 128], NM[:, qc, :], ident)
                return m
            K["nmt"] = tt = pe(go, F[bk], ready["m"])
            F[bk] = t = dve(lambda e: e.tensor_copy(NT[:, :], ps[0:4, bk * 512:(bk + 1) * 512]), tt, K.get("ntd"))
            K["ntd"] = K[("qs", b, hh)] = P.put(
                "sp", lambda e: e.dma_start(QS[16:17, 4 * hh:4 * hh + 4, :].bitcast(f32), NT[:, :].bitcast(f32)),
                t, tt, sem="d_nt", by=16)
            yield

        pxf = [t_rep] * 4
        pxn = [0]

        later = []

        def apply():
            b, hh, sc, j, sl, te = later.pop(0)
            K["pv"] = K[("pv", b)] = pe(lambda e: e.matmul(
                ps[32 * j:32 * j + 32, 7 * 512:8 * 512], vh[:, b % 2, sc, 4 * hh + j, :], PX[:, sl, :],
                start=(sc == 0), stop=(sc == 3), tile_position=(0, 32 * j)), te, F[7] if sc == 0 else None,
                K[("vh", b)])
            pxf[sl] = K["pv"]

        def attend(b, hh):
            for sc in range(4):
                for j in range(4):
                    h = 4 * hh + j
                    bk = 5 + j % 2
                    sl = pxn[0] % 4
                    pxn[0] += 1
                    tp = pe(lambda e, h=h, sc=sc, bk=bk: e.matmul(
                        bank(bk), KS[:, h, 128 * sc:128 * sc + 128], QS[:, h, :], start=True, stop=True),
                        F[bk], K[("qs", b, hh)])
                    F[bk] = te = act(lambda e, bk=bk, sl=sl: e.activation(
                        PX[:, sl, :], bank(bk), ACT.Exp, scale=0.25), tp, pxf[sl])
                    later.append((b, hh, sc, j, sl, te))
                    K[("st", hh)] = tp
                    if sc * 4 + j >= 3:
                        apply()
                    yield

        def tail(b, hh):
            for _ in range(3):
                apply()
                if later and later[0][0:2] == (b, hh):
                    yield
            F[7] = t_o = act(lambda e: e.activation(ox[:, :], bank(7), ACT.Copy), K["pv"], K.get("ox"))
            yield
            yield
            bk = fb()

            def sums(e):
                for c in range(4):
                    m = e.matmul(bank(bk, 4 * c, 4 * c + 4), ox[:, 128 * c:128 * c + 128],
                                 CST[:, C_SEL:C_SEL + 128:32], start=True, stop=True)
                return m
            tb = pe(sums, F[bk], t_o)
            F[bk] = t = dve(lambda e: e.reciprocal(R16[:, :], bank(bk, 0, 16)), tb, K.get("r16"))
            K["r16"] = t = dve(lambda e: e.tensor_copy(
                rc[:, :, :], R16[:, :].unsqueeze(2).broadcast_to([128, 16, 32])), t, K.get("rc"))
            yield
            yield
            b2 = fb()
            K["rc"] = tb = turn(lambda c: rc[:, 4 * c:4 * c + 4, :], b2, t)
            F[b2] = K["ox"] = K[("on", hh)] = dve(lambda e: e.tensor_tensor(on2[:, hh, :], bank(b2), ox[:, :],
                                                                            ALU.mult), tb, K.get("wo"))
            yield

        def post_a(b):
            x = XB[:, b % NXB, :]
            yield
            yield
            bk = fb()

            def wo(e):
                for hh in range(2):
                    m = e.matmul(bank(bk), WO[:, hh, :], on2[:, hh, :], start=(hh == 0), stop=(hh == 1))
                return m
            K["wo"] = tp = pe(wo, F[bk], K[("on", 0)], K[("on", 1)])
            F[bk] = x2[b] = dve(lambda e: e.scalar_tensor_tensor(
                out=x, in0=bank(bk), scalar=bo[:, 0:1], in1=x, op0=ALU.add, op1=ALU.add), tp, t_bo)
            xs[b] = P.put("sp", lambda e: e.dma_start(XD[b, :, :], x), x2[b], sem=f"d_xs{b % 2}", by=16)
            yield

        def post_b(b):
            x = XB[:, b % NXB, :]
            d = b % 2
            x3_ = x3[:, d, :]
            x2[b] = t = yield from norm(x, x3_, 1, ST3[:, b, :], x2[b], K.get(("x3", d)))
            t_x3 = t
            yield
            bk = fb()
            tt = turn(lambda c: x3_[:, c:512:4], bk, t)
            F[bk] = t = act(lambda e: e.activation(x3T[:, :, :], bank(bk), ACT.Copy), tt, K.get("x3T"))
            yield
            bg = fb()

            def gate(e):
                for c in range(4):
                    m = e.matmul(bank(bg, 0, 32), x3T[:, c, :], GW[:, c, :], start=(c == 0), stop=(c == 3))
                return m
            K["x3T"] = tp = pe(gate, F[bg], t)
            dve(lambda e: e.tensor_copy(LM[:, 0:32], bank(bg, 0, 32)), tp)
            t = dve(lambda e: e.tensor_scalar(SG[:, :], bank(bg, 0, 32), -1.0, None, ALU.mult), tp, t_pad)
            F[bg] = t
            t_e = act(lambda e: e.activation(SG[:, :], SG[:, :], ACT.Exp), t)
            L3 = LM[:, 0:32].rearrange("p (g k) -> p g k", k=8)
            t = dve(lambda e: e.tensor_reduce(G[:, 0:4], L3, AX.X, ALU.max), t)
            t = dve(lambda e: e.max(m8[:, :], G[:, :]), t)
            t = dve(lambda e: e.match_replace(G2[:, :], m8[:, :], G[:, :], -BIG), t)
            t = dve(lambda e: e.tensor_scalar(KP[:, :], G2[:, 0:4], -BIG, -1e30, ALU.not_equal, ALU.mult), t)
            t = dve(lambda e: e.tensor_tensor(L3, L3, KP[:, :].unsqueeze(2).broadcast_to([128, 4, 8]), ALU.add), t)
            yield
            t = dve(lambda e: e.max(m8[:, :], LM[:, :]), t)
            t = dve(lambda e: e.match_replace(LM2[:, :], m8[:, :], LM[:, :], -BIG), t)
            t_m = dve(lambda e: e.tensor_scalar(M[:, :], LM2[:, 0:32], -BIG, None, ALU.is_equal), t, K.get("rank"))
            dve(lambda e: e.tensor_tensor(RM[:, 1 - d, :], RM[:, d, :], M[:, :], ALU.add), t_m)
            yield
            t = dve(lambda e: e.tensor_scalar(SG[:, :], SG[:, :], 1.0, None, ALU.add), t_e)
            t = dve(lambda e: e.reciprocal(SG[:, :], SG[:, :]), t)
            t = dve(lambda e: e.scalar_tensor_tensor(out=SG[:, :], in0=SG[:, :], scalar=1.0, in1=M[:, :],
                                                     op0=ALU.mult, op1=ALU.mult, accum_out=SM[:, :]), t)
            t = dve(lambda e: e.reciprocal(SM[:, :], SM[:, :]), t)
            t_w = dve(lambda e: e.tensor_scalar(SG[:, :], SG[:, :], SM[:, 0:1], None, ALU.mult), t)
            yield
            br = fb()

            def rank(e):
                e.matmul(bank(br, 0, 32), CST[:, C_TRI:C_TRI + 128], M[:, :], start=True, stop=False)
                return e.matmul(bank(br, 0, 32), CST[:, C_ONE:C_ONE + 128], RM[:, d, :], start=False, stop=True)
            K["rank"] = tr = pe(rank, F[br], t_m)
            F[br] = t = dve(lambda e: e.tensor_tensor(SV[:, b, :], bank(br, 0, 32), CST[:, C_BA:C_BA + 32], ALU.add), tr)
            t = dve(lambda e: e.tensor_tensor(SV[:, b, :], SV[:, b, :], M[:, :], ALU.mult), t)
            t_s8 = dve(lambda e: e.max(S8[:, :], SV[:, b, :]), t)
            t_si = dve(lambda e: e.tensor_scalar(SI[:, b, :], S8[:, :], -1.0, None, ALU.add), t_s8)
            yield
            jt = [None, None]
            for k in range(6):
                q = k % 2
                jt[q] = dve(lambda e, k=k, q=q: e.scalar_tensor_tensor(
                    out=junk[:, q, :], in0=SV[:, b, :], scalar=S8[:, k:k + 1], in1=SG[:, :],
                    op0=ALU.is_equal, op1=ALU.mult, accum_out=W6[:, b, k:k + 1]), t_s8, t_w, jt[q])
                ts = P.put("pool", lambda e, k=k: e.indirect_dma_start(
                    out=XS[:, :], out_offset=bass.IndirectOffsetOnAxis(ap=SI[:, b, k:k + 1], axis=0),
                    in_=x3_, in_offset=None), t_x3, t_si, zeroed, sem=f"d_sc{d}", by=16)
                yield
            K[("x3", d)] = ts

        def drain(g):
            for _ in g:
                pass

        def weave(rounds, *gens):
            count = [0] * len(gens)
            for k in range(1, rounds + 1):
                for i, (g, n) in enumerate(gens):
                    while count[i] * rounds < k * (n or rounds):
                        count[i] += 1
                        next(g, None)
            for g, n in gens:
                if n is None:
                    drain(g)

        def chain(*gens):
            for g in gens:
                yield from g

        def rest(n):
            for _ in range(n):
                yield

        none = iter(())
        for b in range(4):
            load_x(b)
        load_c(0)
        load_c(1)
        drain(chainA(0))
        drain(prep(0))
        weave(36, (chainA(1), None), (front(0, 0), 18))
        for x_ in range(32):
            zeroed = load("d_z", zrows[x_], zt[:, :], t_z)
        for b in range(NB):
            ga = chainA(b + 2) if b + 2 < NB else iter(())
            more = b + 1 < NB
            weave(20, (chain(tail(b - 1, 1), post_a(b - 1), prep(b + 1) if more else none) if b
                       else prep(1), None),
                  (chain(rest(4), attend(b, 0)), None), (front(b, 1), 20), (ga, AS))
            if b + 4 < NB:
                load_x(b + 4)
            if b + 2 < NB:
                load_c(b + 2)
            weave(20, (chain(tail(b, 0), post_b(b - 1) if b else none), None),
                  (chain(rest(3), attend(b, 1)), None), (front(b + 1, 0) if more else none, 20), (ga, AS))
            drain(ga)
        drain(chain(tail(NB - 1, 1), post_a(NB - 1), post_b(NB - 1)))

        P.fence(*P.last("pe", "act", "dve", "pool", "d_z", "d_cst", "d_xs0", "d_xs1", "d_sc0", "d_sc1"))
        ax.close()

        mo = ExitStack()
        EB = sb(mo, "EB", [1, 128], i32)
        RB = sb(mo, "RB", [1, 128], i32)
        ci = sb(mo, "ci", [128, 32], i32)
        nbf = sb(mo, "nbf", [128, 32])
        cu = sb(mo, "cu", [128, 2, 32])
        cn = sb(mo, "cn", [128, 32])
        st = sb(mo, "st", [128, 32])
        jk = sb(mo, "jk", [128, 4, 32])
        ac = sb(mo, "ac", [128, 4])
        er = sb(mo, "er", [128, 3])
        of = sb(mo, "of", [128, 2, 32])
        sl_ = sb(mo, "sl", [128, NB, 32])
        YI = sb(mo, "YI", [128, NB, 8], i32)
        Q = {}

        def table():
            tr = pe(lambda e: e.matmul(bank(0, 0, 32), CST[:, C_ONE:C_ONE + 128], RM[:, NB % 2, :],
                                       start=True, stop=True), F[0])
            dve(lambda e: e.tensor_copy(cn[:, :], bank(0, 0, 32)), tr)
            F[0] = t = dve(lambda e: e.tensor_scalar(ci[:, :], bank(0, 0, 32), float(BLK - 1), None, ALU.add), tr)
            t = dve(lambda e: e.tensor_scalar(ci[:, :], ci[:, :], 8, None, ALU.logical_shift_right), t)
            t = dve(lambda e: e.tensor_copy(nbf[:, :], ci[:, :]), t)
            t = dve(lambda e: e.tensor_copy(cu[:, 0, :], nbf[:, :]), t)
            for k in range(5):
                s, a, b_ = 1 << k, k % 2, 1 - k % 2
                dve(lambda e, s=s, a=a, b_=b_: e.tensor_copy(cu[:, b_, 0:s], cu[:, a, 0:s]), t)
                t = dve(lambda e, s=s, a=a, b_=b_: e.tensor_tensor(cu[:, b_, s:32], cu[:, a, s:32],
                                                                   cu[:, a, 0:32 - s], ALU.add), t)
            dve(lambda e: e.tensor_scalar(er[:, 2:3], CST[:, C_BI:C_BI + 1], 1.0, cu[:, 1, 31:32], ALU.add, ALU.min), t)
            t = dve(lambda e: e.tensor_tensor(st[:, :], cu[:, 1, :], nbf[:, :], ALU.subtract), t)
            dve(lambda e: e.tensor_scalar(of[:, 0, :], cn[:, :], -float(BLK), 0.0, ALU.add, ALU.max), t)
            dve(lambda e: e.tensor_scalar(of[:, 1, :], nbf[:, :], -1.0, float(BLK), ALU.add, ALU.mult), t)
            for q, (b0, b1) in enumerate(((cu[:, 1, :], CST[:, C_ONE:C_ONE + 32]), (cu[:, 1, :], nbf[:, :]),
                                          (cu[:, 1, :], cn[:, :]), (st[:, :], cn[:, :]))):
                t_ = dve(lambda e, q=q, b0=b0, b1=b1: e.scalar_tensor_tensor(
                    out=jk[:, q, :], in0=b0, scalar=er[:, 2:3], in1=b1, op0=ALU.is_lt, op1=ALU.mult,
                    accum_out=ac[:, q:q + 1]), t)
            dve(lambda e: e.tensor_copy(er[:, 0:1], ac[:, 0:1]), t_)
            t = dve(lambda e: e.tensor_tensor(ac[:, 3:4], ac[:, 3:4], ac[:, 2:3], ALU.subtract), t_)
            t = dve(lambda e: e.tensor_scalar(ac[:, 3:4], ac[:, 3:4], -float(BLK), 0.0, ALU.add, ALU.max), t)
            t_ = dve(lambda e: e.tensor_tensor(ac[:, 1:2], er[:, 2:3], ac[:, 1:2], ALU.subtract), t_)
            t_ = dve(lambda e: e.tensor_scalar(ac[:, 1:2], ac[:, 1:2], -1.0, float(BLK), ALU.add, ALU.mult), t_)
            t = dve(lambda e: e.tensor_tensor(ac[:, 1:2], ac[:, 1:2], ac[:, 3:4], ALU.min), t, t_)
            t = dve(lambda e: e.scalar_tensor_tensor(out=er[:, 1:2], in0=ac[:, 0:1], scalar=float(ROOM),
                                                     in1=ac[:, 1:2], op0=ALU.mult, op1=ALU.add), t)

            def across(e):
                e.transpose(ps[0:1, 0:128], er[:, 0:1], ident)
                return e.transpose(ps[0:1, 128:256], er[:, 1:2], ident)
            tr = pe(across, F[0], t)
            dve(lambda e: e.tensor_copy(EB[:, :], ps[0:1, 0:128]), tr)
            F[0] = Q["eb"] = dve(lambda e: e.tensor_copy(RB[:, :], ps[0:1, 128:256]), tr)

        def slots():
            def over(v):
                return v.unsqueeze(1).broadcast_to([128, NB, 32])
            t = dve(lambda e: e.tensor_tensor(of[:, 1, :], of[:, 1, :], of[:, 0, :], ALU.subtract), Q["eb"])
            dve(lambda e: e.tensor_scalar(st[:, :], st[:, :], float(BLK), 1.0, ALU.mult, ALU.add), Q["eb"])
            t = dve(lambda e: e.tensor_tensor(SV[:, :, :], SV[:, :, :], over(CST[:, C_BA:C_BA + 32]), ALU.subtract), t)
            yield
            t = dve(lambda e: e.tensor_tensor(sl_[:, :, :], SV[:, :, :], over(of[:, 0, :]), ALU.is_ge), t)
            yield
            t = dve(lambda e: e.tensor_tensor(sl_[:, :, :], sl_[:, :, :], over(of[:, 1, :]), ALU.mult), t)
            yield
            t = dve(lambda e: e.tensor_tensor(sl_[:, :, :], sl_[:, :, :], SV[:, :, :], ALU.add), t)
            yield
            t = dve(lambda e: e.tensor_tensor(sl_[:, :, :], sl_[:, :, :], over(st[:, :]), ALU.add), t)
            yield
            t = dve(lambda e: e.scalar_tensor_tensor(out=sl_[:, :, :], in0=SV[:, :, :], scalar=0.0, in1=sl_[:, :, :],
                                                     op0=ALU.is_ge, op1=ALU.mult), t)
            yield
            for n in range(NB):
                t_ = dve(lambda e, n=n: e.max(SV[:, n, 0:8], sl_[:, n, :]), t)
                if n % 4 == 3:
                    yield
            Q["yi"] = dve(lambda e: e.tensor_scalar(YI[:, :, :], SV[:, :, 0:8], -1.0, None, ALU.add), t_)

        WL = sb(mo, "WL", [128, 2, 2, 4, 352])
        DL = sb(mo, "DL", [128, 2, 3, 512])
        WG = [sb(mo, f"WG{i}", [128, 2, 2, 4, 352], f32r) for i in range(2)]
        WD = [sb(mo, f"WD{i}", [128, 2, 3, 512], f32r) for i in range(2)]
        NX = 3
        XI = sb(mo, "XI", [128, NX, 2, 512])
        XC = sb(mo, "XC", [128, 2, 512])
        XT = sb(mo, "XT", [128, 2, 2, 512], f32r)
        HS = sb(mo, "HS", [128, 2, 352])
        HT = sb(mo, "HT", [128, 2, 2, 384], f32r)
        YO = sb(mo, "YO", [128, 3, 2, 512])
        xif, xtf, yof = [None] * NX, [None] * 2, [None] * 3
        hsf, htf = [None, None], [None, None]
        sets = ["s0", "s1"] + list(range(NBLK)) + ["s0", "s1"]
        items = [("s", n, s, s) for n in range(PRE) for s in range(2)] + \
                [("m", b, i, b + 2) for b in range(NBLK) for i in range(2)] + \
                [("s", n, s, NBLK + 2 + s) for n in range(PRE, NB) for s in range(2)]
        N = len(items)
        last_use = {}
        for n, it in enumerate(items):
            last_use[it[3]] = n
        tin, txT, th, tht, src, xq = {}, {}, {}, {}, {}, {}
        tland, twt, tdone, tused = {}, {}, {}, {}
        landf = [[], []]
        regs = {}
        cnt = {"x": 0, "t": 0, "y": 0}
        slotted = []

        def land(k):
            q = k % 2
            if k >= len(sets):
                return
            w = sets[k]
            parts = []
            if isinstance(w, str):
                s = int(w[1])
                for i, name in enumerate(("sw_gate", "sw_up")):
                    parts.append(lambda e, i=i, name=name: e.dma_start(
                        WL[:, q, i, :, :], I[name][:, 352 * s:352 * s + 352].rearrange("(p c) n -> p c n", c=4)))
                parts.append(lambda e: e.dma_start(
                    DL[:, q, 0:2, :], I["sw_down"][352 * s:352 * s + 256, :].rearrange("(c p) n -> p c n", p=128)))
                parts.append(lambda e: e.dma_start(DL[0:96, q, 2, :], I["sw_down"][352 * s + 256:352 * s + 352, :]))
            else:
                def gate(e):
                    regs[w] = e.value_load(EB[0:1, w:w + 1], min_val=0, max_val=31)
                    return e.dma_start(WL[:, q, 0, :, :], I["w_gate"][bass.ds(regs[w], 1), :, :]
                                       .rearrange("a (p c) n -> p (a c) n", c=4))
                parts.append(gate)
                parts.append(lambda e: e.dma_start(WL[:, q, 1, :, :], I["w_up"][bass.ds(regs[w], 1), :, :]
                                                   .rearrange("a (p c) n -> p (a c) n", c=4)))
                parts.append(lambda e: e.dma_start(DL[:, q, 0:2, :], I["w_down"][bass.ds(regs[w], 1), 0:256, :]
                                                   .rearrange("a (c p) n -> p (a c) n", p=128)))
                parts.append(lambda e: e.dma_start(DL[0:96, q, 2, :], I["w_down"][bass.ds(regs[w], 1), 256:352, :]
                                                   .rearrange("a p n -> p (a n)")))
            for go in parts:
                tland[k] = P.put("sp", go, Q.get("eb") if not isinstance(w, str) else None, *landf[q],
                                 sem=f"d_wt{q}", by=16)

        def split(k):
            if k >= len(sets):
                return
            q = k % 2
            t0 = tland[k]
            free = tused[k - 2] if k >= 2 else None
            for w in range(2):
                for c in range(0, 4, 2):
                    ta = act(lambda e, w=w, c=c: e.activation(WG[q][:, 0, w, c:c + 2, :], WL[:, q, w, c:c + 2, :],
                                                              ACT.Copy), t0, free)
                    yield
                    tb = dve(lambda e, w=w, c=c: e.tensor_tensor(
                        WG[q][:, 1, w, c:c + 2, :], WL[:, q, w, c:c + 2, :],
                        WG[q][:, 0, w, c:c + 2, :].bitcast(f32), ALU.subtract), ta)
                    yield
            free = tdone[k - 2] if k >= 2 else None
            for r, c0, c1 in ((128, 0, 2), (96, 2, 3)):
                ta = act(lambda e, r=r, c0=c0, c1=c1: e.activation(WD[q][0:r, 0, c0:c1, :], DL[0:r, q, c0:c1, :],
                                                                   ACT.Copy), free)
                yield
                tb = dve(lambda e, r=r, c0=c0, c1=c1: e.tensor_tensor(
                    WD[q][0:r, 1, c0:c1, :], DL[0:r, q, c0:c1, :], WD[q][0:r, 0, c0:c1, :].bitcast(f32),
                    ALU.subtract), ta)
                yield
            twt[k] = (ta, tb)
            landf[q] = [ta, tb]

        def fetch(n):
            kind, a, i, k = items[n]
            if i == 1:
                src[n], tin[n] = src[n - 1], tin[n - 1]
                return
            sl = src[n] = cnt["x"] % NX
            cnt["x"] += 1
            if kind == "s":
                tin[n] = load(f"d_xi{sl}", XI[:, sl, 0, :], XD[a, :, :], xif[sl])
            else:
                def go(e):
                    r = e.value_load(RB[0:1, a:a + 1], min_val=0, max_val=NROW - BLK)
                    return e.dma_start(XI[:, sl, :, :], XS[bass.ds(r, BLK), :].rearrange("(i p) d -> p i d", p=128))
                tin[n] = P.put("sp", go, xif[sl], Q["eb"], sem=f"d_xi{sl}", by=16)

        def s1(n):
            kind, a, i, k = items[n]
            if kind == "s" and i == 1:
                txT[n], xq[n] = txT[n - 1], xq[n - 1]
                return
            q = xq[n] = cnt["t"] % 2
            cnt["t"] += 1
            sl = src[n]
            rows, t = XI[:, sl, i, :], tin[n]
            if kind == "s":
                rows = XC[:, q, :]
                t = dve(lambda e: e.tensor_scalar(rows, XI[:, sl, 0, :], ST3[:, a, 0:1], ST3[:, a, 1:2],
                                                  ALU.subtract, ALU.mult), t, xcf[q])

            def go(e):
                for c in range(4):
                    m = e.transpose(bank(q, 128 * c, 128 * c + 128), rows[:, c:512:4], ident)
                return m
            tt = pe(go, F[q], t)
            if kind == "s":
                xcf[q] = tt
            elif i == 1:
                xif[sl] = tt
            ta = act(lambda e: e.activation(XT[:, q, 0, :], bank(q), ACT.Copy), tt, xtf[q])
            F[q] = tb = dve(lambda e: e.tensor_tensor(XT[:, q, 1, :], bank(q), XT[:, q, 0, :].bitcast(f32),
                                                      ALU.subtract), ta)
            txT[n] = tb

        xcf = [None, None]

        def three(e, out_, lh, rh, first, last):
            e.matmul(out_, lh(0), rh(0), start=first, stop=False)
            e.matmul(out_, lh(0), rh(1), start=False, stop=False)
            return e.matmul(out_, lh(1), rh(0), start=False, stop=last)

        def s2(n):
            kind, a, i, k = items[n]
            q = n % 2
            bg, bu = 2 + q, 4 + q

            def go(e):
                for w in range(2):
                    for c in range(4):
                        m = three(e, bank(bg if w == 0 else bu, 0, 352),
                                  lambda p: XT[:, xq[n], p, 128 * c:128 * c + 128],
                                  lambda p: WG[k % 2][:, p, w, c, :], c == 0, c == 3)
                return m
            tp = pe(go, F[bg], F[bu], txT[n], *twt[k])
            xtf[xq[n]] = tp
            if last_use[k] == n:
                tused[k] = tp
            tg = act(lambda e: e.activation(HS[:, q, :], bank(bg, 0, 352), ACT.Silu), tp, hsf[q])
            F[bg] = tg
            th[n] = dve(lambda e: e.tensor_tensor(HS[:, q, :], bank(bu, 0, 352), HS[:, q, :], ALU.mult), tg)
            F[bu] = th[n]

        def s3(n):
            q = n % 2

            def go(e):
                for c in range(3):
                    r = 128 if c < 2 else 96
                    m = e.transpose(ps[0:r, 6 * 512 + 128 * c:6 * 512 + 128 * c + 128],
                                    HS[:, q, 128 * c:128 * c + r], ident)
                return m
            tt = pe(go, F[6], th[n])
            hsf[q] = tt
            for r, a, b in ((128, 0, 256), (96, 256, 384)):
                ta = act(lambda e, r=r, a=a, b=b: e.activation(
                    HT[0:r, q, 0, a:b], ps[0:r, 6 * 512 + a:6 * 512 + b], ACT.Copy), tt, htf[q])
            for r, a, b in ((128, 0, 256), (96, 256, 384)):
                tht[n] = dve(lambda e, r=r, a=a, b=b: e.tensor_tensor(
                    HT[0:r, q, 1, a:b], ps[0:r, 6 * 512 + a:6 * 512 + b], HT[0:r, q, 0, a:b].bitcast(f32),
                    ALU.subtract), ta)
            F[6] = tht[n]

        def s4(n):
            kind, a, i, k = items[n]
            q = n % 2

            def go(e):
                for c in range(3):
                    r = 128 if c < 2 else 96
                    m = three(e, bank(7), lambda p: HT[0:r, q, p, 128 * c:128 * c + 128],
                              lambda p: WD[k % 2][0:r, p, c, :],
                              c == 0 and not (kind == "s" and i == 1), c == 2 and not (kind == "s" and i == 0))
                return m
            tp = pe(go, F[7] if not (kind == "s" and i == 1) else None, tht[n])
            htf[q] = tp
            if last_use[k] == n:
                tdone[k] = tp
            if kind == "s" and i == 0:
                return
            yq = cnt["y"] % 3
            if kind == "s":
                sl = src[n]
                xif[sl] = F[7] = dve(lambda e: e.tensor_tensor(YO[:, yq, 0, :], bank(7), XI[:, sl, 0, :], ALU.add),
                                     tp, yof[yq])
                yd[a] = yof[yq] = P.put("act", lambda e: e.dma_start(YD[a, :, :], YO[:, yq, 0, :]), F[7],
                                        sem=f"d_y{yq}", by=16)
            else:
                F[7] = dve(lambda e: e.tensor_copy(YO[:, yq, i, :], bank(7)), tp, yof[yq] if i == 0 else None)
                if i == 0:
                    return

                yof[yq] = P.put("pool", lambda e: e.dma_start(
                    YS[BLK * a:BLK * a + BLK, :].rearrange("(i p) d -> p i d", p=128), YO[:, yq, :, :]), F[7],
                    sem=f"d_yb{yq}", by=16)
                if a == NBLK - 1:
                    stored.extend(P.last(*[f"d_yb{q}" for q in range(3)]))
            cnt["y"] += 1

        yd, stored = {}, []

        def combine():
            tg = {}

            def gather(g):
                n, k, sl = g // 6, g % 6, g % NG
                tg[g] = P.put("pool", lambda e: e.indirect_dma_start(
                    out=GB[:, sl, :], out_offset=None, in_=YS[:, :],
                    in_offset=bass.IndirectOffsetOnAxis(ap=YI[:, n, k:k + 1], axis=0)),
                    gf[sl], Q["yi"], *stored, sem=f"d_g{sl}", by=16)

            def residual(n):
                tc[n] = load(f"d_cx{n % NC}", CB[:, n % NC, :], YD[n, :, :], yd[n], cbf[n % NC])

            def finish(n):
                cbf[n % NC] = P.put("sp", lambda e: e.dma_start(out[n, :, :], CB[:, n % NC, :]), tc[n],
                                    sem=f"d_out{n % NC}", by=16)

            tc = {}
            for g in range(LAG):
                gather(g)
            residual(0)
            for n in range(NB):
                xs_ = n % NC
                for k in range(6):
                    g = 6 * n + k
                    sl = g % NG
                    if k == 3:
                        if n:
                            finish(n - 1)
                        while n + 1 < NB and n + 1 not in yd:
                            yield
                        if n + 1 < NB:
                            residual(n + 1)
                    if g + LAG < 6 * NB:
                        gather(g + LAG)
                    tc[n] = gf[sl] = dve(lambda e, n=n, k=k, sl=sl, xs_=xs_: e.scalar_tensor_tensor(
                        out=CB[:, xs_, :], in0=GB[:, sl, :], scalar=W6[:, n, k:k + 1], in1=CB[:, xs_, :],
                        op0=ALU.mult, op1=ALU.add), tg[g], tc[n])
                    yield
            finish(NB - 1)

        NG, LAG, NC = 8, 6, 3
        GB = sb(mo, "GB", [128, NG, 512])
        CB = sb(mo, "CB", [128, NC, 512])
        gf, cbf = [None] * NG, [None] * NC

        land(0)
        land(1)
        for k in range(2):
            for _ in split(k):
                pass
        nf = 0

        def ahead(n):
            nonlocal nf
            while nf < min(n, N):
                fetch(nf)
                nf += 1
        ahead(2)
        s1(0)
        cb = None

        def combined(steps):
            for _ in range(steps if cb is not None else 0):
                next(cb, None)

        spl = iter(())
        mid = 2 * PRE
        for n in range(N + 1):
            if n == 1:
                table()
                yi = slots()
                land(2)
                land(3)
            ahead(n + 4)
            if n < N and items[n][0] == "m" and items[n][2] == 0:
                k = items[n][3]
                for _ in spl:
                    pass
                spl = split(k + 1)
                if k + 2 not in tland:
                    land(k + 2)
            if n + 1 < N:
                s1(n + 1)
            combined(2)
            if n >= 1:
                s3(n - 1)
            for _ in range(3):
                next(spl, None)
            if n < N:
                k = items[n][3]
                if k not in twt:
                    for _ in spl:
                        pass
                if k not in twt:
                    if k not in tland:
                        land(k)
                    for _ in split(k):
                        pass
                s2(n)
            for _ in range(3):
                next(spl, None)
            if n >= 1:
                s4(n - 1)
            if n == mid - 1:
                for _ in split(2):
                    pass
            if n > mid:
                next(yi, None)
            if stored and cb is None:
                cb = combine()
            combined(2)
        for _ in cb:
            pass
        for xs_ in range(NC):
            P.quiet("sp", lambda e, t=cbf[xs_]: e.wait_ge(sems[t[0]], t[1]))
        mo.close()

        sems = {k: top.enter_context(nc.semaphore("s_" + k)) for k in P.count}
        block = top.enter_context(nc.Block())

        @block.tensor
        def _(e):
            P.emit("pe", e, sems)

        @block.scalar
        def _(e):
            P.emit("act", e, sems)

        @block.vector
        def _(e):
            P.emit("dve", e, sems)

        @block.gpsimd
        def _(e):
            P.emit("pool", e, sems)

        @block.sync
        def _(e):
            P.emit("sp", e, sems)


def constants():
    c = np.zeros((128, C_N), np.float32)
    p = np.arange(128)
    c[:, C_ID:C_ID + 128] = np.eye(128)
    c[:, C_TRI:C_TRI + 128] = p[:, None] < p[None, :]
    c[:, C_ONE:C_ONE + 128] = 1.0
    c[:, C_SEL:C_SEL + 128] = p[:, None] == (p[None, :] // 32) * 32 + 16
    inv = (np.float32(1.0) / np.float32(10000.0) ** (np.arange(0, 16, 2, dtype=np.float32) / np.float32(16))
           ).astype(np.float32)
    pos = (np.arange(512, dtype=np.float32)[:, None] * inv[None, :]).astype(np.float32)
    cos, sin = np.cos(pos).astype(np.float32), np.sin(pos).astype(np.float32)
    for r in range(128):
        d = r % 16
        c[r, C_COS:C_COS + 512] = cos[:, d % 8]
        c[r, C_SIN:C_SIN + 512] = -sin[:, d % 8] if d < 8 else sin[:, d % 8]
    c[:, C_MSK:C_MSK + 128] = np.where(p[None, :] > p[:, None], -1e30, 0.0)
    c[:, C_AB] = p % 32 < 16
    c[:, C_AB + 1] = p % 32 >= 16
    c[16, C_AB + 2] = 1.0
    c[:, C_BI] = p
    c[:, C_BA:C_BA + 32] = np.arange(32)[None, :] * ROOM + 1
    return c


def spreading():
    r = np.zeros((128, 8, 320), np.float32)
    for h in range(8):
        for n, on in enumerate(SPREAD):
            for d in range(16 if on else 0):
                r[16 * h + d, h, 32 * n + d] = 1.0
    return r


def laid_out(inputs):
    g = {k: np.asarray(v) for k, v in inputs.items()}
    swap = np.concatenate([np.arange(8, 16), np.arange(0, 8)])
    Wk, Wq = g["L0_xattn_Wk"], g["L0_xattn_Wq"]
    wx = np.zeros((128, 4, 128), np.float32)
    bx = np.zeros((128, 7), np.float32)
    wv = np.zeros((128, 256), np.float32)
    wo = np.zeros((128, 2, 128), np.float32)
    turned = (np.arange(8)[:, None] * 16 + swap[None, :]).ravel()
    for kq, (W, b) in enumerate(((Wk, g["L0_xattn_bk"]), (Wq, g["L0_xattn_bq"]))):
        for pm, r in enumerate((np.arange(128), turned)):
            wx[:, 2 * kq + pm, :] = W[r, :].T
            bx[:, 2 * kq + pm] = b[r]
    for hh in range(2):
        for j in range(4):
            rows = 16 * (4 * hh + j) + np.arange(16)
            wv[:, 128 * hh + 32 * j:128 * hh + 32 * j + 16] = g["L0_xattn_Wv"][rows, :].T
            wo[32 * j:32 * j + 16, hh, :] = g["L0_xattn_Wo"][:, rows].T
            bx[32 * j:32 * j + 16, 4 + hh] = g["L0_xattn_bv"][rows]
    bx[:, 6] = g["L0_xattn_bo"]
    a = {
        "x": g["x"], "ctx": g["ctx_2048"], "cst": constants(), "rep": spreading(), "wx": wx, "wv": wv, "wo": wo, "bx": bx,
        "Wq": g["L0_attn_Wq"], "Wk": g["L0_attn_Wk"], "Wv": g["L0_attn_Wv"], "Wo": g["L0_attn_Wo"],
        "lq": np.stack([g["L0_attn_lq1"], g["L0_attn_lk1"], g["L0_attn_lq2"], g["L0_attn_lk2"]]),
        "gate_w": g["L0_ffn_gate_w"], "w_gate": g["L0_ffn_w_gate"], "w_up": g["L0_ffn_w_up"],
        "w_down": g["L0_ffn_w_down"], "sw_gate": g["L0_ffn_sw_gate"], "sw_up": g["L0_ffn_sw_up"],
        "sw_down": g["L0_ffn_sw_down"],
    }
    return {k: np.ascontiguousarray(v) for k, v in a.items()}


def kernel(**inputs):
    import concourse.bacc as bacc
    from concourse.bass_utils import run_bass_kernel_spmd

    nc = bacc.Bacc("TRN2", target_bir_lowering=False, num_devices=1)
    arrays, aps = {}, {}
    for name, a in laid_out(inputs).items():
        arrays[f"in_{name}"] = a
        aps[name] = nc.dram_tensor(f"in_{name}", a.shape, mybir.dt.from_np(a.dtype), kind="ExternalInput").ap()
    out = nc.dram_tensor("out_0", (NB, 128, 512), mybir.dt.float32, kind="ExternalOutput").ap()
    build(nc, aps, out)
    r = run_bass_kernel_spmd(nc, [arrays], core_ids=[0])
    return r.results[0]["out_0"]
```
